# Optimizing a Trainium2 kernel written in Bass

```python
import numpy as np
import jax
import jax.numpy as jnp

def _softmax(x, axis=-1):
    return jax.nn.softmax(x, axis=axis)

def _gelu(x):
    return jax.nn.gelu(x, approximate=True)

def _silu(x):
    return jax.nn.silu(x)

def _sigmoid(x):
    return jax.nn.sigmoid(x)

def _layernorm(x, axis=-1, eps=1e-05):
    m = jnp.mean(x, axis=axis, keepdims=True)
    v = jnp.var(x, axis=axis, keepdims=True)
    return (x - m) / jnp.sqrt(v + eps)

def _scatter_add(tgt, idx, src, axis=0):
    return tgt.at[idx].add(src)

def _segment_sum(src, seg, n):
    return jax.ops.segment_sum(src, seg, n)
kernel_name = 'mk_gnn_resnorm_d1_gnn_r16_c835c6'

def setup_inputs(seed: int=0):
    np.random.seed(seed)
    _w = jnp.asarray

    def _rec_inputs():
        import jax
        import jax.numpy as jnp
        _gk = jax.random.key(seed)
        x = -0.0006008 + 1.001 * jax.random.normal(jax.random.fold_in(_gk, 1), (6250, 256), jnp.float32)
        src = jax.random.randint(jax.random.fold_in(_gk, 2), (100000,), 0, 6250, jnp.int32)
        dst = jnp.minimum((6250 * jax.random.uniform(jax.random.fold_in(_gk, 3), (100000,)) ** 2.0).astype(jnp.int32), 99999)
        _o = jnp.argsort(dst, stable=True)
        src = src[_o]
        dst = dst[_o]
        edge_attr_32 = 0.000398968 + 1.00027 * jax.random.normal(jax.random.fold_in(_gk, 11), (100000, 32), jnp.float32)
        edge_type_3 = jax.random.randint(jax.random.fold_in(_gk, 13), (100000,), 0, 3, jnp.int32)
        return (x, src, dst, edge_attr_32, edge_type_3)
    x, src, dst, edge_attr_32, edge_type_3 = _rec_inputs()

    def _L0_gnn_setup():
        import jax, jax.numpy as jnp
        import numpy as np
        N_NODES = 625
        N_EDGES = 10000
        D = 256
        NUM_REL = 3
        NUM_DISTS = 32
        N_LAYERS = 3

        def _gcn_forward(x, edge_index, edge_type, edge_attr, weights, roots, biases, edge_w, edge_b):
            n = x.shape[0]
            src, dst = (edge_index[0], edge_index[1])
            ew = edge_attr @ edge_w + edge_b
            rel_masks = [(edge_type == i).astype(x.dtype) for i in range(NUM_REL)]
            inv_cnt = [1.0 / jnp.maximum(jax.ops.segment_sum(m, dst, num_segments=n), 1.0) for m in rel_masks]
            for l in range(N_LAYERS):
                residual = x
                msg = jax.nn.relu(x[src] * ew)
                out = jnp.zeros((n, D), dtype=x.dtype)
                for i in range(NUM_REL):
                    h = jax.ops.segment_sum(msg * rel_masks[i][:, None], dst, num_segments=n)
                    h = h * inv_cnt[i][:, None]
                    out = out + h @ weights[l, i]
                out = out + x @ roots[l] + biases[l]
                x = residual + jax.nn.relu(out)
            return x
        key = jax.random.key(seed)
        ks = jax.random.split(key, 12)
        s = 1.0 / np.sqrt(D)
        inp = {'x': jax.random.normal(ks[0], (N_NODES, D), dtype=jnp.float32), 'edge_index': jax.random.randint(ks[1], (2, N_EDGES), 0, N_NODES, dtype=jnp.int32), 'edge_type': jax.random.randint(ks[2], (N_EDGES,), 0, NUM_REL, dtype=jnp.int32), 'edge_attr': jax.random.normal(ks[3], (N_EDGES, NUM_DISTS), dtype=jnp.float32), 'weights': jax.random.normal(ks[4], (N_LAYERS, NUM_REL, D, D), dtype=jnp.float32) * s, 'roots': jax.random.normal(ks[5], (N_LAYERS, D, D), dtype=jnp.float32) * s, 'biases': jax.random.normal(ks[6], (N_LAYERS, D), dtype=jnp.float32) * 0.01, 'edge_w': jax.random.normal(ks[7], (NUM_DISTS, D), dtype=jnp.float32) * (1.0 / np.sqrt(NUM_DISTS)), 'edge_b': jax.random.normal(ks[8], (D,), dtype=jnp.float32) * 0.01}
        return inp
    _L0_gnn_all = _L0_gnn_setup()
    _L0_gnn_in = {k: v for k, v in _L0_gnn_all.items() if k in ('weights', 'roots', 'biases', 'edge_w', 'edge_b')}
    del _L0_gnn_all
    return {'x': x, 'src': src, 'dst': dst, 'edge_attr_32': edge_attr_32, 'edge_type_3': edge_type_3, 'L0_gnn_weights': _L0_gnn_in['weights'], 'L0_gnn_roots': _L0_gnn_in['roots'], 'L0_gnn_biases': _L0_gnn_in['biases'], 'L0_gnn_edge_w': _L0_gnn_in['edge_w'], 'L0_gnn_edge_b': _L0_gnn_in['edge_b']}

def reference(x, src, dst, edge_attr_32, edge_type_3, L0_gnn_weights, L0_gnn_roots, L0_gnn_biases, L0_gnn_edge_w, L0_gnn_edge_b):
    import jax
    import jax.numpy as jnp

    def _L0_gnn_ref(x, edge_index, edge_type, edge_attr, weights, roots, biases, edge_w, edge_b):
        import jax, jax.numpy as jnp
        import numpy as np
        N_NODES = 625
        N_EDGES = 10000
        D = 256
        NUM_REL = 3
        NUM_DISTS = 32
        N_LAYERS = 3

        def _gcn_forward(x, edge_index, edge_type, edge_attr, weights, roots, biases, edge_w, edge_b):
            n = x.shape[0]
            src, dst = (edge_index[0], edge_index[1])
            ew = edge_attr @ edge_w + edge_b
            rel_masks = [(edge_type == i).astype(x.dtype) for i in range(NUM_REL)]
            inv_cnt = [1.0 / jnp.maximum(jax.ops.segment_sum(m, dst, num_segments=n), 1.0) for m in rel_masks]
            for l in range(N_LAYERS):
                residual = x
                msg = jax.nn.relu(x[src] * ew)
                out = jnp.zeros((n, D), dtype=x.dtype)
                for i in range(NUM_REL):
                    h = jax.ops.segment_sum(msg * rel_masks[i][:, None], dst, num_segments=n)
                    h = h * inv_cnt[i][:, None]
                    out = out + h @ weights[l, i]
                out = out + x @ roots[l] + biases[l]
                x = residual + jax.nn.relu(out)
            return x
        return _gcn_forward(x, edge_index, edge_type, edge_attr, weights, roots, biases, edge_w, edge_b)
    edge_index = jnp.stack([src, dst])
    x = _layernorm(x + _L0_gnn_ref(x, edge_index, edge_type_3, edge_attr_32, L0_gnn_weights, L0_gnn_roots, L0_gnn_biases, L0_gnn_edge_w, L0_gnn_edge_b), axis=-1)
    return x

_drawn_inputs = setup_inputs


def setup_inputs(seed=0):
    import zlib

    import numpy as np

    out = dict(_drawn_inputs(seed))
    spreads = {}
    factors = {'L0_gnn_biases': 8.0, 'L0_gnn_edge_b': 8.0}
    for name, (base, spread) in spreads.items():
        noise = np.random.default_rng([zlib.crc32(name.encode()), seed]).standard_normal(out[name].shape)
        drawn = base * np.exp(spread * noise) if base else spread * noise
        out[name] = jnp.asarray(drawn.astype(out[name].dtype))
    for name, factor in factors.items():
        out[name] = (out[name] * factor).astype(out[name].dtype)
    return out
```

```python
import concourse.bass as bass
from concourse import mybir
from contextlib import ExitStack


def block_starts(l):
    last, out = -4, []
    for k in range(49):
        if l == 0:
            q = 394 + 3 * k
        else:
            tiles = min(782.0, 782.0 * (128 * (k + 1) / 6250.0) ** 0.5 + 6)
            q = max(int(tiles) // 2 + 4, last + 4)
            q += q % 2
            if k == 48:
                q = max(q, 394)
        out.append(q)
        last = q
    return out


def block_limits():
    import numpy as np

    limits = np.zeros(7 * 128, np.float32)
    for l in range(1, 3):
        for k, q in enumerate(block_starts(l)):
            j = min(782, 2 * (q - 2))
            limits[j:] = np.maximum(limits[j:], 128 * (k + 1))
    limits[782:] = 0
    return np.ascontiguousarray(limits.reshape(7, 128).T)


def gnn_program(nc, x_in, src, dst, edge_attr, edge_type, weights, roots, biases, edge_w, edge_b, due, out):
    F32, BF16, I32 = mybir.dt.float32, mybir.dt.bfloat16, mybir.dt.int32
    ALU = mybir.AluOpType
    ACT = mybir.ActivationFunctionType
    AX = mybir.AxisListType
    DVE = mybir.EngineType.DVE

    N, E, D, R, L = 6250, 100000, 256, 3, 3
    NT = 782
    LAST = E - 128 * (NT - 1)
    NP = NT // 2
    CH = 7
    CL = NT - 128 * (CH - 1)
    WN = 32
    WK = WN * R
    ACC = N * R + WK
    NB = 49
    NLAST = N - 128 * (NB - 1)
    NG = NQ = 196
    XR, SR, TR, AR = 10, 8, 3, 6
    XB, XT, TB = 3, 2, 4
    PAD = 1000000

    x1 = nc.dram_tensor("x1", (N, D), F32).ap()
    x2 = nc.dram_tensor("x2", (N, D), F32).ap()
    attr_t = nc.dram_tensor("attr_t", (NG, 96, 512), BF16).ap()
    HR = 128 * R * NB
    sums = nc.dram_tensor("sums", (HR + 128, D), F32).ap()
    xs = [x_in, x1, x2, out]

    def rows(k):
        return 128 if k < NB - 1 else NLAST

    def tiles_of(g):
        return 4 if g < NG - 1 else NT - 4 * (NG - 1)

    def ring(l, i, depth, per):
        n = l * per + i
        return n % depth, n // depth + 1

    ctx = ExitStack()
    with ctx:
        def sb(name, shape, dt=F32):
            return ctx.enter_context(nc.sbuf_tensor(name, shape, dt))

        def sem(name):
            return ctx.enter_context(nc.semaphore(name))

        def sems(name, n):
            return [sem(f"{name}{i}") for i in range(n)]

        acc = sb("acc", [128, 2, ACC])
        accf = acc[:, :, :].rearrange("p h k -> p (h k)")
        idx = sb("idx", [128, NT], I32)
        kr = sb("kr", [128, NT])
        lo = sb("lo", [128, NT])
        hb = sb("hb", [128, NT])
        xg = sb("xg", [128, XR, D])
        S = sb("S", [128, SR, WK])
        at = sb("at", [128, TR, 512], BF16)
        an = sb("an", [128, 3, 4, 32])
        hs = sb("hs", [128, 2, 4, 96], BF16)
        W = sb("W", [128, 8, D])
        bias = sb("bias", [128, D])
        wsb = sb("wsb", [128, 3, D], BF16)
        iota = sb("iota", [128, 147], BF16)
        ident = sb("ident", [128, 128])
        identb = sb("identb", [128, 128], BF16)
        oh_a = sb("oh_a", [128, AR, 128], BF16)
        oh_b = sb("oh_b", [128, AR, 147], BF16)
        inv = sb("inv", [128, 147])
        cnt = hb[:, 2 * D:2 * D + 147]
        diff = sb("diff", [128, 128])
        brow = sb("brow", [1, 128 * CH], I32)
        base = sb("base", [128, CH])
        duet = sb("duet", [128, CH])
        bad = sb("bad", [128, 2])
        flag = sb("flag", [1, 1], I32)
        zcol = sb("zcol", [128, 1])
        ones = sb("ones", [128, 1])
        eps = sb("eps", [128, 1])
        xblk = sb("xblk", [128, XB, D])
        xT = sb("xT", [128, XT, D])
        t = sb("t", [128, TB, D])
        x0b = hb[:, 0:2 * D].rearrange("p (i d) -> p i d", i=2)
        bst = sb("bst", [128, 2, 6])
        mv = sb("mv", [128, 2, 2])
        sd = sb("sd", [128, 2, 1])
        rs = sb("rs", [128, 2, 1])

        P0 = 2 * ACC - 7 * 896 - D
        prep = [accf[:, P0 + 896 * i:P0 + 896 * (i + 1)] for i in range(7)]
        p_dst, p_typ, p_src = (p.bitcast(I32) for p in prep[0:3])
        p_f, p_rel, p_lo, p_hb = prep[3:7]
        p_ew = accf[:, P0 + 7 * 896:P0 + 7 * 896 + D]

        def c3(p):
            return p.rearrange("q (c p) -> q c p", p=128)

        bank = [ctx.enter_context(nc.psum_tensor(f"bank{i}", [128, 512], F32)) for i in range(8)]
        pE = bank[0:2]
        pA = bank[2:4]
        pT = bank[4]
        pTb = bank[4][:, :].bitcast(BF16)
        pH = bank[5]
        pD = bank[6:8]

        s_pad, s_cst, s_id, s_idb, s_zc, s_one, s_ez = (sem(n) for n in (
            "s_pad", "s_cst", "s_id", "s_idb", "s_zc", "s_one", "s_ez"))
        s_src, s_dst, s_typ, s_ew, s_due = (sem(n) for n in ("s_src", "s_dst", "s_typ", "s_eww", "s_due"))
        s_pf, s_pt, s_pc, s_idx, s_pca, s_wsb = (sem(n) for n in ("s_pf", "s_pt", "s_pc", "s_idx", "s_pca", "s_wsb"))
        s_ch = sem("s_ch")
        s_z0 = sem("s_z0")
        s_flag = sem("s_flag")
        s_g = sems("s_g", XR)
        s_e, s_m, s_r, s_S, s_sc, s_acc = (sem(n) for n in ("s_e", "s_m", "s_r", "s_S", "s_sc", "s_acc"))
        s_an = sems("s_an", 3)
        s_h = sems("s_h", 3)
        s_res, s_tr, s_atc = sem("s_res"), sem("s_tr"), sem("s_atc")
        s_ao = sems("s_ao", TR)
        s_at = sems("s_at", TR)
        s_oa, s_ob, s_hc, s_cd, s_cm, s_df = (sem(n) for n in (
            "s_oa", "s_ob", "s_hc", "s_cd", "s_cm", "s_df"))
        s_w = sem("s_w")
        s_xl = sems("s_xl", XB)
        s_x0 = sems("s_x0", 2)
        s_xt, s_xc, s_d0, s_d1, s_f0, s_f1, s_dn, s_z = (sem(n) for n in (
            "s_xt", "s_xc", "s_d0", "s_d1", "s_f0", "s_f1", "s_dn", "s_z"))
        s_dc = sems("s_dc", TB)
        s_st, s_sq = sem("s_st"), sem("s_sq")
        s_xo = sems("s_xo", TB)

        producers = {"load": ("sync", 16), "swdge0": ("gpsimd", 16), "swdge1": ("gpsimd", 16),
                     "swdge2": ("gpsimd", 16), "pool": ("gpsimd", 1), "act": ("scalar", 1),
                     "pe": ("tensor", 1), "dve": ("vector", 1)}
        s_gen = {p: sem(f"s_gen_{p}") for p in producers}
        s_turn = {p: sem(f"s_turn_{p}") for p in ("sync", "gpsimd", "scalar", "tensor", "vector")}

        block = ctx.enter_context(nc.Block())

        def uses(l, i, depth, per):
            return len(range(i, l * per, depth))

        def starting(l, q, lag):
            return [k for k in range(NB) if starts[l][k] + lag == q]

        def acc_by(l, k):
            return min(NT, 2 * (starts[l][k] - 2))

        def slot(l, j):
            return 4 * ((l * NQ + j // 4) % (SR // 4)) + j % 4

        starts = [block_starts(l) for l in range(L)]
        ends = [starts[l][-1] + 15 for l in range(L)]

        G_x, G_sum = xg[:, 0, :], xg[:, 3, :]
        G_w, G_at = xg[0:33, 1, :], xg[0:33, 2, 0:128]
        G_eq, G_eqb, G_tri = xg[:, 4, 0:128], xg[:, 4, 128:256], xg[:, 5, 0:128]
        G_h = xg[:, 6:9, :]
        G_key, G_lo, G_hb, G_bef, G_ok, G_row, G_dump = (xg[:, 9, c:c + 1] for c in range(7))
        G_inv = xg[:, 9, 8:11]
        G_src, G_dst = (xg[:, 9, c:c + 1].bitcast(I32) for c in (12, 13))
        G_an = an[:, 0, 0, :]
        G_T = t[:, 0:4, :].rearrange("p a (b c) -> p (a b) c", c=128)
        G_t, G_x0, G_xb = xT[:, 0, :], xT[:, 1, :], xblk[:, 0, :]
        G_pk, G_pc = bank[0][:, 256:384], pH[:, 0:147]

        def start_steps():
            return [
                ("load", lambda e, i: e.dma_start(G_w[0:32, :], edge_w)),
                ("load", lambda e, i: e.dma_start(G_w[32:33, :], edge_b.rearrange("(a n) -> a n", a=1))),
                ("dve", lambda e, i: e.memset(G_at[32:33, :], 1.0)),
                ("dve", lambda e, i: e.memset(G_an, 0.0)),
                ("dve", lambda e, i: e.memset(inv[:, :], 0.0)),
                ("pool", lambda e, i: e.memset(G_tri, 1.0)),
                ("pool", lambda e, i: e.affine_select(out=G_tri, in_=G_tri, compare_op=ALU.is_gt, fill=0.0, base=0,
                                                      pattern=[[-1, 128]], channel_multiplier=1)),
                ("pool", lambda e, i: e.iota(G_dump, [[0, 1]], base=HR, channel_multiplier=1,
                                             allow_small_or_imprecise_dtypes=True)),
            ]

        def layer_steps(l):
            half = (HR + 128) // 2
            zero = [("load", lambda e, i, h=h: e.dma_start(
                sums[half * h:half * (h + 1), :].rearrange("(p r) d -> p (r d)", p=128),
                accf[:, 0:half * D // 128])) for h in range(2)]
            return zero + [("load", lambda e, i, r=r: e.dma_start(
                W[:, 2 * r:2 * r + 2, :],
                (weights[l, r] if r < R else roots[l]).rearrange("(h p) o -> p h o", p=128))) for r in range(R + 1)] + [
                ("load", lambda e, i: e.dma_start(bias[:, :], biases[l:l + 1, :].broadcast_to([128, D])))]

        def col(a, i):
            return a[:, i:i + 1] if isinstance(i, int) else a[:, bass.ds(i, 1)]

        def edge_steps(l, n):
            steps = [
                ("load", lambda e, i: e.dma_start(G_an[0:n, :], edge_attr[bass.ds(i * 128, n), :])),
                ("pe", lambda e, i: e.transpose(pT[0:32, 0:128], G_an, ident[:, :])),
                ("act", lambda e, i: e.activation(G_at[0:32, :], pT[0:32, 0:128], ACT.Copy)),
                ("pe", lambda e, i: e.matmul(pE[0][:, 0:256], G_at, G_w, start=True, stop=True)),
                ("dve", lambda e, i: e.tensor_copy(G_src, col(idx, i))),
                ("dve", lambda e, i: e.tensor_copy(G_lo, col(lo, i))),
                ("dve", lambda e, i: e.tensor_copy(G_hb, col(hb, i))),
                (f"swdge{l}", lambda e, i: e.indirect_dma_start(
                    out=G_x, out_offset=None, in_=xs[l],
                    in_offset=bass.IndirectOffsetOnAxis(ap=G_src, axis=0))),
                ("dve", lambda e, i: e.tensor_tensor(G_x, G_x, pE[0][:, 0:256], ALU.mult)),
                ("act", lambda e, i: e.activation(G_x, G_x, ACT.Relu)),
                ("dve", lambda e, i: e.scalar_tensor_tensor(G_key, G_hb, 128.0, G_lo, ALU.mult, ALU.subtract)),
                ("dve", lambda e, i: e.tensor_scalar(G_key, G_key, 0.5, None, ALU.add)),
                ("pe", lambda e, i: e.matmul(G_pk, G_key.to_broadcast([128, 128]), ident[:, :],
                                             start=True, stop=True)),
                ("dve", lambda e, i: e.tensor_scalar(G_eq, G_pk, G_key, None, ALU.is_equal)),
                ("dve", lambda e, i: e.tensor_tensor(G_eqb, G_eq, G_tri, ALU.mult)),
                ("dve", lambda e, i: e.tensor_reduce(G_bef, G_eqb, AX.X, ALU.add)),
                ("dve", lambda e, i: e.tensor_scalar(G_ok, G_key, float(HR), None, ALU.is_lt)),
                ("dve", lambda e, i: e.scalar_tensor_tensor(G_ok, G_bef, 0.5, G_ok, ALU.is_lt, ALU.mult)),
                ("dve", lambda e, i: e.tensor_tensor(G_row, G_key, G_dump, ALU.subtract)),
                ("dve", lambda e, i: e.tensor_tensor(G_row, G_row, G_ok, ALU.mult)),
                ("dve", lambda e, i: e.tensor_tensor(G_row, G_row, G_dump, ALU.add)),
                ("dve", lambda e, i: e.tensor_copy(G_dst, G_row)),
                ("pe", lambda e, i: e.matmul(pA[0][:, 0:256], G_eq, G_x, start=True, stop=True)),
                ("act", lambda e, i: e.activation(G_sum, pA[0][:, 0:256], ACT.Copy)),
                (f"swdge{l}", lambda e, i: e.indirect_dma_start(
                    out=sums, out_offset=bass.IndirectOffsetOnAxis(ap=G_dst, axis=0), in_=G_sum, in_offset=None,
                    compute_op=ALU.add, oob_is_err=True)),
            ]
            if l == 0:
                steps += [
                    ("dve", lambda e, i: e.tensor_scalar(oh_a[:, 0, :], iota[:, 0:128], G_lo, 0.5, ALU.add,
                                                         ALU.is_equal)),
                    ("dve", lambda e, i: e.tensor_scalar(oh_b[:, 0, :], iota[:, :], G_hb, None, ALU.is_equal)),
                    ("pe", lambda e, i: e.matmul(G_pc, oh_a[:, 0, :], oh_b[:, 0, :], start=True, stop=True)),
                    ("dve", lambda e, i: e.tensor_tensor(inv[:, :], inv[:, :], G_pc, ALU.add)),
                ]
            return steps

        def count_steps():
            return [
                ("dve", lambda e, i: e.tensor_scalar(inv[:, :], inv[:, :], 1.0, None, ALU.max)),
                ("dve", lambda e, i: e.reciprocal(inv[:, :], inv[:, :])),
            ]

        def turn_all(e, n):
            for h in range(2):
                e.transpose(bank[0][:, 128 * h:128 * h + n], G_xb[0:n, 128 * h:128 * h + 128], ident[0:n, 0:n])
            for m in range(2, 8):
                ins = e.transpose(bank[m // 4][:, 128 * (m % 4):128 * (m % 4) + 128],
                                  G_h[:, m // 2 - 1, 128 * (m % 2):128 * (m % 2) + 128], ident[:, :])
            return ins

        def mix_all(e, n):
            for m in range(4):
                for h in range(2):
                    ins = e.matmul(pD[m // 2][0:n, 256 * (m % 2):256 * (m % 2) + 256], G_T[:, 2 * m + h, 0:n],
                                   W[:, 2 * ((m - 1) % 4) + h, :], start=(h == 0), stop=(h == 1))
            return ins

        def node_steps(l, n):
            tt = G_t[0:n, :]
            steps = [
                ("load", lambda e, i: e.dma_start(G_h, sums[bass.ds(i * (3 * 128), 3 * 128), :]
                                                  .rearrange("(r p) d -> p r d", p=128))),
                ("load", lambda e, i: e.dma_start(G_xb[0:n, :], xs[l][bass.ds(i * 128, n), :])),
                ("pe", lambda e, i: turn_all(e, n)),
                ("act", lambda e, i: e.activation(G_T[:, 0:2, 0:n], bank[0][:, 0:256]
                                                  .rearrange("p (a c) -> p a c", c=128)[:, :, 0:n], ACT.Copy)),
                ("act", lambda e, i: e.activation(G_T[:, 2:4, :], bank[0][:, 256:512]
                                                  .rearrange("p (a c) -> p a c", c=128), ACT.Copy)),
                ("act", lambda e, i: e.activation(G_T[:, 4:8, :], bank[1][:, :]
                                                  .rearrange("p (a c) -> p a c", c=128), ACT.Copy)),
                ("pe", lambda e, i: mix_all(e, n)),
                ("dve", lambda e, i: e.tensor_copy(G_inv, inv[:, bass.ds(i * 3, 3)])),
                ("dve", lambda e, i: e.tensor_tensor(tt, pD[0][0:n, 0:256], bias[0:n, :], ALU.add)),
            ] + [
                ("dve", lambda e, i, m=m: e.scalar_tensor_tensor(
                    tt, pD[m // 2][0:n, 256 * (m % 2):256 * (m % 2) + 256], G_inv[0:n, m - 1:m], tt,
                    ALU.mult, ALU.add)) for m in (1, 2, 3)
            ] + [
                ("dve", lambda e, i: e.scalar_tensor_tensor(tt, tt, 0.0, G_xb[0:n, :], ALU.max, ALU.add)),
            ]
            if l == L - 1:
                b, m, d, r = bst[0:n, 0, :], mv[0:n, 0, :], sd[0:n, 0, :], rs[0:n, 0, :]
                steps += [
                    ("load", lambda e, i: e.dma_start(G_x0[0:n, :], x_in[bass.ds(i * 128, n), :])),
                    ("dve", lambda e, i: e.tensor_tensor(tt, tt, G_x0[0:n, :], ALU.add)),
                    ("dve", lambda e, i: e.bn_stats(b, tt)),
                    ("dve", lambda e, i: e.bn_aggr(m, b)),
                    ("act", lambda e, i: e.activation(d, m[:, 1:2], ACT.Sqrt, bias=eps[0:n, :])),
                    ("dve", lambda e, i: e.reciprocal(r, d)),
                    ("dve", lambda e, i: e.tensor_scalar(tt, tt, m[:, 0:1], r, ALU.subtract, ALU.mult)),
                ]
            return steps + [("load", lambda e, i: e.dma_start(xs[l + 1][bass.ds(i * 128, n), :], tt))]

        def general(eng, name):
            done = dict.fromkeys(producers, 0)
            last = [None]

            def phase(steps, i0=0, times=1):
                per = {p: producers[p][1] * sum(s[0] == p for s in steps) for p in producers}

                def issue(i, turn):
                    now = dict(done)
                    prev = (steps[-1][0], now[steps[-1][0]] + turn * per[steps[-1][0]])
                    for p, step in steps:
                        now[p] += producers[p][1]
                        if producers[p][0] == name:
                            eng.wait_ge(s_gen[prev[0]], prev[1])
                            eng.sem_inc(s_turn[name], 1)
                            step(eng, i).then_inc(s_gen[p], producers[p][1])
                        prev = (p, now[p] + turn * per[p])

                mine = any(producers[p][0] == name for p, _ in steps)
                if producers[steps[0][0]][0] == name and last[0]:
                    eng.wait_ge(s_gen[last[0]], done[last[0]])
                if mine and times == 1:
                    issue(i0, 0)
                elif mine:
                    with eng.Fori(i0, i0 + times) as i:
                        issue(i, i - i0)
                for p in producers:
                    done[p] += times * per[p]
                last[0] = steps[-1][0]

            phase(start_steps())
            for l in range(L):
                phase(layer_steps(l))
                phase(edge_steps(l, 128))
                phase(edge_steps(l, 128), 1, NT - 2)
                phase(edge_steps(l, LAST), NT - 1)
                if l == 0:
                    phase(count_steps())
                phase(node_steps(l, 128), 0, NB - 1)
                phase(node_steps(l, NLAST), NB - 1)
            if name == "sync":
                eng.wait_ge(s_gen["load"], done["load"])
                for l in range(L):
                    eng.wait_ge(s_gen[f"swdge{l}"], done[f"swdge{l}"])

        def both(eng, name, fast):
            eng.wait_ge(s_flag, 3)
            late = eng.value_load(flag[0:1, 0:1], min_val=0, max_val=128 * 128 * CH + 128 * CH)
            with eng.If(late == 0):
                fast()
            with eng.Else():
                general(eng, name)

        @block.sync
        def _(eng):
            eng.wait_ge(s_pad, 3)
            for p, a, s in ((p_src, src, s_src), (p_dst, dst, s_dst), (p_typ, edge_type, s_typ)):
                eng.dma_start(c3(p)[:, 0:CH - 1, :],
                              a[0:128 * 128 * (CH - 1)].rearrange("(c q p) -> q c p", q=128, p=128)).then_inc(s, 16)
                eng.dma_start(c3(p)[0:CL - 1, CH - 1, :],
                              a[128 * 128 * (CH - 1):128 * (NT - 1)].rearrange("(q p) -> q p", p=128)).then_inc(s, 16)
                eng.dma_start(c3(p)[CL - 1:CL, CH - 1, 0:LAST],
                              a[128 * (NT - 1):E].rearrange("(q p) -> q p", q=1)).then_inc(s, 16)
            eng.wait_ge(s_ez, 1)
            for i in range(3):
                eng.dma_start(p_ew[32 * i:32 * i + 32, :], edge_w).then_inc(s_ew, 16)
            eng.dma_start(p_ew[96:97, :], edge_b.rearrange("(a n) -> a n", a=1)).then_inc(s_ew, 16)
            eng.dma_start(duet[:, :], due).then_inc(s_due, 16)

            def load_weights(l):
                if l:
                    eng.wait_ge(s_dn, NB * l)
                for i in range(R):
                    eng.dma_start(W[:, 2 * i:2 * i + 2, :],
                                  weights[l, i].rearrange("(h p) o -> p h o", p=128)).then_inc(s_w, 16)
                eng.dma_start(W[:, 6:8, :], roots[l].rearrange("(h p) o -> p h o", p=128)).then_inc(s_w, 16)
                eng.dma_start(bias[:, :], biases[l:l + 1, :].broadcast_to([128, D])).then_inc(s_w, 16)

            def load_attr(g):
                if g >= 3:
                    eng.wait_ge(s_h[2], g - 2)
                if g < NG - 1:
                    eng.dma_start(an[:, g % 3, :, :], edge_attr[512 * g:512 * (g + 1), :]
                                  .rearrange("(j p) d -> p j d", p=128)).then_inc(s_an[g % 3], 16)
                else:
                    eng.dma_start(an[:, g % 3, 0, :], edge_attr[512 * g:512 * g + 128, :]).then_inc(s_an[g % 3], 16)
                    eng.dma_start(an[0:LAST, g % 3, 1, :], edge_attr[128 * (NT - 1):E, :]).then_inc(s_an[g % 3], 16)

            def keep_attr(g):
                w = 128 * tiles_of(g)
                eng.wait_ge(s_atc, g + 1)
                eng.dma_start(attr_t[g, :, 0:w], at[0:96, g % TR, 0:w]).then_inc(s_ao[g % TR], 16)

            def reload_attr(l, g):
                G = l * NG + g
                eng.wait_ge(s_e, l * NP + 2 * max(0, g - TR + 1))
                w = 128 * tiles_of(g)
                eng.dma_start(at[0:96, G % TR, 0:w], attr_t[g, :, 0:w]).then_inc(s_at[G % TR], 16)

            def load_x(l, k):
                K, n = NB * l + k, rows(k)
                if K >= XB:
                    eng.wait_ge(s_dn, K - XB + 1)
                eng.dma_start(xblk[0:n, K % XB, :], xs[l][128 * k:128 * k + n, :]).then_inc(s_xl[K % XB], 16)

            def load_x0(k):
                n = rows(k)
                if k >= 2:
                    eng.wait_ge(s_dn, NB * (L - 1) + k - 1)
                eng.dma_start(x0b[0:n, k % 2, :], x_in[128 * k:128 * k + n, :]).then_inc(s_x0[k % 2], 16)

            def store(l, k):
                K, n = NB * l + k, rows(k)
                eng.wait_ge(s_dn, K + 1)
                eng.dma_start(xs[l + 1][128 * k:128 * k + n, :], t[0:n, K % TB, :]).then_inc(s_xo[K % TB], 16)

            def fast():
                for g in range(3):
                    load_attr(g)
                for l in range(L):
                    late = 8 if l < L - 1 else 13
                    for q in range(-4, ends[l]):
                        if l == 0 and q % 2 == 0:
                            if 3 <= q // 2 + 4 < NG:
                                load_attr(q // 2 + 4)
                            if 0 <= q // 2 < NG:
                                keep_attr(q // 2)
                        if l and q % 2 == 0 and q // 2 + 2 < NG:
                            reload_attr(l, q // 2 + 2)
                        if q == 0:
                            for i in range(TB if l else 0):
                                eng.wait_ge(s_xo[i], 16 * uses(l, i, TB, NB))
                            load_weights(l)
                            for k in range(XB):
                                load_x(l, k)
                            if l == L - 1:
                                load_x0(0)
                                load_x0(1)
                        for k in starting(l, q, late):
                            store(l, k)
                            if k + XB < NB:
                                load_x(l, k + XB)
                            if l == L - 1 and k + 2 < NB:
                                load_x0(k + 2)
                    if l == 0:
                        for i in range(TR):
                            eng.wait_ge(s_ao[i], 16 * uses(1, i, TR, NG))
                for i in range(TB):
                    eng.wait_ge(s_xo[i], 16 * uses(L, i, TB, NB))

            both(eng, "sync", fast)

        @block.gpsimd
        def _(eng):
            eng.memset(c3(p_src)[:, CH - 1, :], 0).then_inc(s_pad, 1)
            eng.memset(c3(p_dst)[:, CH - 1, :], PAD).then_inc(s_pad, 1)
            eng.memset(c3(p_typ)[:, CH - 1, :], 0).then_inc(s_pad, 1)
            eng.memset(zcol[:, :], 0.0).then_inc(s_zc, 1)
            eng.memset(p_ew, 0.0).then_inc(s_ez, 1)
            eng.memset(ident[:, :], 0.0).then_inc(s_id, 1)
            eng.wait_ge(s_id, 1)
            eng.affine_select(out=ident[:, :], in_=ident[:, :], compare_op=ALU.not_equal, fill=1.0,
                              base=0, pattern=[[-1, 128]], channel_multiplier=1).then_inc(s_id, 1)
            eng.iota(iota[:, :], [[1, 147]], base=0, channel_multiplier=0,
                     allow_small_or_imprecise_dtypes=True).then_inc(s_cst, 1)
            eng.memset(ones[:, :], 1.0).then_inc(s_cst, 1)
            eng.memset(eps[:, :], 1e-5).then_inc(s_cst, 1)
            eng.memset(accf[:, 24000:P0], 0.0).then_inc(s_z0, 1)
            eng.memset(diff[:, :], 0.0).then_inc(s_df, 1)
            for i, (fill, b) in enumerate(((0.5, 0), (-0.5, 1), (0.5, -127))):
                eng.wait_ge(s_df, i + 1)
                eng.affine_select(out=diff[:, :], in_=diff[:, :], compare_op=ALU.not_equal, fill=fill,
                                  base=b, pattern=[[-1, 128]], channel_multiplier=1).then_inc(s_df, 1)
            eng.wait_ge(s_idx, 2)
            def fast():
                for l in range(L):
                    if l:
                        for i in range(TB):
                            eng.wait_ge(s_xo[i], 16 * uses(l, i, TB, NB))
                    for j in range(NT):
                        n = l * NT + j
                        if n >= XR:
                            eng.wait_ge(s_sc, 2 * ((n - XR) // 2 + 1))
                        eng.indirect_dma_start(
                            out=xg[:, n % XR, :], out_offset=None, in_=xs[l],
                            in_offset=bass.IndirectOffsetOnAxis(ap=idx[:, j:j + 1], axis=0)).then_inc(s_g[n % XR], 16)

            both(eng, "gpsimd", fast)

        @block.scalar
        def _(eng):
            eng.wait_ge(s_zc, 1)
            for a in range(0, 24000, 6000):
                eng.activation(accf[:, a:a + 6000], zcol[:, 0:1].to_broadcast([128, 6000]), ACT.Copy).then_inc(s_z0, 1)
            eng.wait_ge(s_id, 2)
            eng.activation(identb[:, :], ident[:, :], ACT.Copy).then_inc(s_idb, 1)

            def copies(dstn, b0, b1):
                eng.activation(dstn[:, 0:512], b0[:, 0:512], ACT.Copy).then_inc(s_pca, 1)
                eng.activation(dstn[:, 512:NT], b1[:, 0:NT - 512], ACT.Copy).then_inc(s_pca, 1)

            eng.wait_ge(s_pt, 3)
            copies(lo, bank[4], bank[5])
            eng.wait_ge(s_pt, 4)
            copies(hb, bank[6], bank[7])

            def part(g, i):
                if i == 0:
                    eng.wait_ge(s_an[g % 3], 16 * (g // 3 + 1) + (16 if g == NG - 1 else 0))
                    if g >= 2:
                        eng.wait_ge(s_tr, g - 1)
                else:
                    eng.wait_ge(s_res, 2 * g + i)
                eng.activation(hs[:, g % 2, :, 32 * i:32 * i + 32], an[:, g % 3, :, :], ACT.Copy).then_inc(s_h[i], 1)

            def attr_copy(g):
                w = 128 * tiles_of(g)
                eng.wait_ge(s_tr, g + 1)
                if g >= TR:
                    eng.wait_ge(s_e, 2 * (g - TR + 1))
                    eng.wait_ge(s_ao[g % TR], 16 * (g // TR))
                eng.activation(at[0:96, g % TR, 0:w], pTb[0:96, 0:w], ACT.Copy).then_inc(s_atc, 1)

            def root(k):
                par, n = k % 2, rows(k)
                eng.wait_ge(s_st, k + 1)
                eng.activation(sd[0:n, par, :], mv[0:n, par, 1:2], ACT.Sqrt, bias=eps[0:n, :]).then_inc(s_sq, 1)

            def fast():
                for l in range(L):
                    for q in range(-6, ends[l]):
                        Q = l * NP + q
                        if l == 0:
                            g = (q + 6) // 2
                            if q % 2 == 0:
                                if g < NG:
                                    part(g, 0)
                                if 0 <= g - 1 < NG:
                                    part(g - 1, 2)
                                if 0 <= g - 2 < NG:
                                    attr_copy(g - 2)
                            else:
                                if g < NG:
                                    part(g, 1)
                        if l == 0 and 0 <= q < NP:
                            for j in (2 * q, 2 * q + 1):
                                if j >= AR:
                                    eng.wait_ge(s_hc, j - AR + 1)
                                eng.activation(oh_a[:, j % AR, :], iota[:, 0:128], ACT.Sign,
                                               bias=lo[:, j:j + 1]).then_inc(s_oa, 1)
                        if 0 <= q < NP:
                            eng.wait_ge(s_m, Q + 1)
                            v = xg[:, (2 * Q) % XR:(2 * Q) % XR + 2, :]
                            eng.activation(v, v, ACT.Relu).then_inc(s_r, 1)
                        for k in starting(l, q, 0):
                            K, n = NB * l + k, rows(k)
                            eng.wait_ge(s_xt, K + 1)
                            if K >= XT:
                                eng.wait_ge(s_d0, K - XT + 1)
                            eng.activation(xT[:, K % XT, :].rearrange("p (h n) -> p h n", h=2)[:, :, 0:n],
                                           pT[:, 0:256].rearrange("p (h n) -> p h n", h=2)[:, :, 0:n],
                                           ACT.Copy).then_inc(s_xc, 1)
                        if l < L - 1:
                            for k in starting(l, q, 4):
                                eng.wait_ge(s_d1, NB * l + k + 1)
                                b = 384 * (k + 1) if k < NB - 1 else ACC
                                eng.activation(acc[:, :, 384 * k:b], zcol[:, 0:1].unsqueeze(2)
                                               .to_broadcast([128, 2, b - 384 * k]), ACT.Copy).then_inc(s_z, 1)
                        else:
                            for k in starting(l, q, 9):
                                root(k)

            both(eng, "scalar", fast)

        @block.tensor
        def _(eng):
            eng.wait_ge(s_id, 2)

            def turn(p, b0, b1):
                for c in range(CH):
                    q = 128 if c < CH - 1 else CL
                    b = b0 if c < 4 else b1
                    last = eng.transpose(b[:, 128 * (c % 4):128 * (c % 4) + q], c3(p)[0:q, c, :], ident[0:q, 0:q])
                last.then_inc(s_pt, 1)

            eng.wait_ge(s_pf, 1)
            turn(p_f, bank[0], bank[1])
            eng.wait_ge(s_pf, 2)
            turn(p_rel, bank[2], bank[3])
            eng.wait_ge(s_pf, 3)
            turn(p_lo, bank[4], bank[5])
            eng.wait_ge(s_pf, 4)
            turn(p_hb, bank[6], bank[7])
            eng.wait_ge(s_idx, 2)
            eng.wait_ge(s_pf, 5)
            eng.wait_ge(s_cst, 2)
            for c in range(CH):
                eng.matmul(bank[c // 4][0:1, 128 * (c % 4):128 * (c % 4) + 128], base[:, c:c + 1], ident[:, :],
                           start=True, stop=True)
            eng.matmul(bank[1][0:1, 510:511], bad[:, 0:1], ones[:, :], start=True, stop=False)
            eng.matmul(bank[1][0:1, 510:511], bad[:, 1:2], ones[:, :], start=False, stop=True).then_inc(s_pt, 1)
            eng.wait_ge(s_flag, 3)
            eng.wait_ge(s_pc, 2)
            eng.wait_ge(s_pca, 4)
            eng.wait_ge(s_wsb, 3)
            eng.wait_ge(s_one, 1)
            eng.wait_ge(s_idb, 1)

            def attr_turn(g):
                eng.wait_ge(s_h[2], g + 1)
                if g >= 1:
                    eng.wait_ge(s_atc, g)
                for i in range(tiles_of(g)):
                    last = eng.transpose(pTb[0:96, 128 * i:128 * i + 128], hs[:, g % 2, i, :], identb[:, :])
                last.then_inc(s_tr, 1)

            def edge_weights(l, q):
                Q = l * NP + q
                g = q // 2
                sl, times = ring(l, g, TR, NG)
                if q % 2 == 0:
                    if l == 0:
                        eng.wait_ge(s_atc, g + 1)
                    else:
                        eng.wait_ge(s_at[sl], 16 * (times - uses(1, sl, TR, NG)))
                if Q >= 2:
                    eng.wait_ge(s_m, Q - 1)
                for i in range(2):
                    c = 256 * (q % 2) + 128 * i
                    for p in range(3):
                        last = eng.matmul(pE[Q % 2][:, 256 * i:256 * i + 256], at[:, sl, c:c + 128], wsb[:, p, :],
                                          start=(p == 0), stop=(p == 2))
                last.then_inc(s_e, 1)

            def collect(l, q):
                V = l * NP + q
                eng.wait_ge(s_r, V + 1)
                if V >= 2:
                    eng.wait_ge(s_acc, 2 * (V - 1))
                eng.wait_ge(s_S, q // 2 + 1 + l * NQ)
                for i in range(2):
                    n = 2 * V + i
                    for h in range(2):
                        last = eng.matmul(pA[V % 2][:, 192 * i + 96 * h:192 * i + 96 * h + 96],
                                          xg[:, n % XR, 128 * h:128 * h + 128], S[:, slot(l, 2 * q + i), :],
                                          start=True, stop=True)
                    last.then_inc(s_sc, 1)
                    if l == 0:
                        eng.wait_ge(s_oa, n + 1)
                        eng.wait_ge(s_ob, n + 1)
                        eng.matmul(pH[:, 0:147], oh_a[:, n % AR, :], oh_b[:, n % AR, :],
                                   start=(n == 0), stop=(n == NT - 1)).then_inc(s_hc, 1)

            def turn_x(l, k):
                K, n = NB * l + k, rows(k)
                eng.wait_ge(s_xl[K % XB], 16 * (K // XB + 1))
                if K:
                    eng.wait_ge(s_xc, K)
                if l == 0:
                    eng.wait_ge(s_atc, min(NG, (starts[l][k] + 2) // 2 + 1))
                for h in range(2):
                    last = eng.transpose(pT[:, 128 * h:128 * h + n], xblk[0:n, K % XB, 128 * h:128 * h + 128],
                                         ident[0:n, 0:n])
                last.then_inc(s_xt, 1)

            def mix(l, k, m):
                K, n = NB * l + k, rows(k)
                o = pD[m // 2][0:n, 256 * (m % 2):256 * (m % 2) + 256]
                if m == 0:
                    eng.wait_ge(s_xc, K + 1)
                    eng.wait_ge(s_f0, K)
                    if k == 0:
                        eng.wait_ge(s_w, 80 * (l + 1))
                if m == 1:
                    eng.wait_ge(s_acc, l * NT + acc_by(l, k))
                if m == 2:
                    eng.wait_ge(s_f1, K)
                for h in range(2):
                    r = m - 1
                    a = (acc[:, h, 384 * k + r:384 * k + r + 3 * (n - 1) + 1:3] if m
                         else xT[:, K % XT, 128 * h:128 * h + n])
                    last = eng.matmul(o, a, W[:, 2 * (r % 4) + h, :], start=(h == 0), stop=(h == 1))
                if m % 2:
                    last.then_inc(pair_done[m // 2], 1)

            pair_done = [s_d0, s_d1]
            def fast():
                for l in range(L):
                    for q in range(-3, ends[l]):
                        if 0 <= q < NP:
                            edge_weights(l, q)
                        for k in starting(l, q, 1):
                            mix(l, k, 0)
                            mix(l, k, 1)
                        if l == 0 and q % 2 and (q + 3) // 2 < NG:
                            attr_turn((q + 3) // 2)
                        for k in starting(l, q, 2):
                            mix(l, k, 2)
                        for k in starting(l, q, 3):
                            mix(l, k, 3)
                        if 0 <= q - 2 < NP:
                            collect(l, q - 2)
                        if l == 0 and q == NP + 2:
                            eng.wait_ge(s_cd, 1)
                            eng.wait_ge(s_df, 4)
                            eng.matmul(pH[:, 256:403], diff[:, :], cnt, start=True, stop=True).then_inc(s_cm, 1)
                        for k in starting(l, q, 0):
                            turn_x(l, k)

            both(eng, "tensor", fast)

        @block.vector
        def _(eng):
            chain = [0]

            def link(ins):
                chain[0] += 1
                ins.then_inc(s_ch, 1)
                eng.wait_ge(s_ch, chain[0])

            eng.memset(at[96:128, :, :], 1.0).then_inc(s_one, 1)
            eng.wait_ge(s_src, 48)
            eng.tensor_copy(p_f, p_src).then_inc(s_pf, 1)
            eng.wait_ge(s_pt, 1)
            eng.tensor_copy(idx[:, 0:512], bank[0][:, 0:512]).then_inc(s_idx, 1)
            eng.tensor_copy(idx[:, 512:NT], bank[1][:, 0:NT - 512]).then_inc(s_idx, 1)
            eng.wait_ge(s_dst, 48)
            eng.wait_ge(s_typ, 48)
            link(eng.tensor_copy(p_f, p_dst))
            link(eng.tensor_reduce(base[:, :], c3(p_f), AX.X, ALU.min))
            link(eng.tensor_tensor(c3(p_lo), c3(p_f), base[:, :].unsqueeze(2).to_broadcast([128, CH, 128]),
                                   ALU.subtract))
            link(eng.scalar_tensor_tensor(p_rel, p_lo, 3.0, p_typ, ALU.mult, ALU.add))
            eng.sem_inc(s_pf, 1)
            link(eng.tensor_scalar(p_hb, p_lo, float(PAD) / 2, None, ALU.is_lt))
            link(eng.scalar_tensor_tensor(p_hb, p_lo, float(WN), p_hb, ALU.is_ge, ALU.mult))
            link(eng.tensor_reduce(bad[:, 0:1], p_hb, AX.X, ALU.add))
            eng.wait_ge(s_due, 16)
            link(eng.tensor_tensor(duet[:, :], base[:, :], duet[:, :], ALU.is_lt))
            link(eng.tensor_reduce(bad[:, 1:2], duet[:, :], AX.X, ALU.add))
            link(eng.tensor_scalar(p_src, p_dst, 127, None, ALU.bitwise_and))
            link(eng.tensor_scalar(p_lo, p_src, -1.0, 0.5, ALU.mult, ALU.add))
            eng.sem_inc(s_pf, 1)
            link(eng.tensor_scalar(p_src, p_dst, 7, None, ALU.logical_shift_right))
            link(eng.scalar_tensor_tensor(p_hb, p_src, 3.0, p_typ, ALU.mult, ALU.add))
            eng.sem_inc(s_pf, 1)
            eng.sem_inc(s_pf, 1)
            eng.wait_ge(s_ew, 64)
            for p in range(3):
                eng.tensor_copy(wsb[:, p, :], p_ew).then_inc(s_wsb, 1)
                if p < 2:
                    eng.wait_ge(s_wsb, p + 1)
                    link(eng.tensor_tensor(p_ew, p_ew, wsb[:, p, :], ALU.subtract))
            eng.wait_ge(s_pt, 2)
            eng.tensor_copy(kr[:, 0:512], bank[2][:, 0:512]).then_inc(s_pc, 1)
            eng.tensor_copy(kr[:, 512:NT], bank[3][:, 0:NT - 512]).then_inc(s_pc, 1)
            eng.wait_ge(s_pt, 5)
            eng.tensor_scalar(brow[:, 0:512], bank[0][0:1, 0:512], 3.0, None, ALU.mult).then_inc(s_flag, 1)
            eng.tensor_scalar(brow[:, 512:896], bank[1][0:1, 0:384], 3.0, None, ALU.mult).then_inc(s_flag, 1)
            eng.tensor_copy(flag[:, :], bank[1][0:1, 510:511]).then_inc(s_flag, 1)
            eng.wait_ge(s_wsb, 3)
            link(eng.memset(accf[:, P0:2 * ACC], 0.0))
            eng.wait_ge(s_z0, 5)
            eng.wait_ge(s_cst, 3)
            eng.wait_ge(s_pca, 4)
            eng.wait_ge(s_flag, 3)
            eng.wait_ge(s_pc, 2)

            def selectors(l, q):
                j, w = 2 * q, min(4, NT - 2 * q)
                at4 = slot(l, j)
                if l or j >= SR:
                    eng.wait_ge(s_sc, l * NT + (j - 4 if j >= SR else 0 if j else -2))
                eng.tensor_tensor(S[:, at4:at4 + w, :], iota[:, 0:WK].unsqueeze(1).to_broadcast([128, w, WK]),
                                  kr[:, j:j + w].unsqueeze(2).to_broadcast([128, w, WK]),
                                  ALU.is_equal).then_inc(s_S, 1)

            def block_ops(l, k):
                K, n = NB * l + k, rows(k)
                i = K % TB
                tt = t[0:n, i, :]

                def wait_own():
                    eng.wait_ge(s_dc[i], steps[i])

                def op(ins):
                    steps[i] += 1
                    ins.then_inc(s_dc[i], 1)

                def mean(r):
                    m = r + 1
                    return eng.scalar_tensor_tensor(tt, pD[m // 2][0:n, 256 * (m % 2):256 * (m % 2) + 256],
                                                    inv[0:n, 3 * k + r:3 * k + r + 1], tt, ALU.mult, ALU.add)

                def first():
                    eng.wait_ge(s_d0, K + 1)
                    eng.wait_ge(s_xo[i], 16 * (K // TB))
                    op(eng.tensor_tensor(tt, pD[0][0:n, 0:256], bias[0:n, :], ALU.add))

                def mean0():
                    wait_own()
                    mean(0).then_inc(s_f0, 1)

                def mean1():
                    eng.wait_ge(s_f0, K + 1)
                    eng.wait_ge(s_d1, K + 1)
                    op(mean(1))

                def mean2():
                    wait_own()
                    mean(2).then_inc(s_f1, 1)

                def residual():
                    eng.wait_ge(s_f1, K + 1)
                    ins = eng.scalar_tensor_tensor(tt, tt, 0.0, xblk[0:n, K % XB, :], ALU.max, ALU.add)
                    if l < L - 1:
                        ins.then_inc(s_dn, 1)
                    else:
                        op(ins)

                def add_x():
                    wait_own()
                    eng.wait_ge(s_x0[k % 2], 16 * (k // 2 + 1))
                    op(eng.tensor_tensor(tt, tt, x0b[0:n, k % 2, :], ALU.add))

                def stats():
                    wait_own()
                    op(eng.bn_stats(bst[0:n, k % 2, :], tt))

                def aggr():
                    wait_own()
                    if k >= 2:
                        eng.wait_ge(s_sq, k - 1)
                    eng.bn_aggr(mv[0:n, k % 2, :], bst[0:n, k % 2, :]).then_inc(s_st, 1)

                def recip():
                    eng.wait_ge(s_sq, k + 1)
                    op(eng.reciprocal(rs[0:n, k % 2, :], sd[0:n, k % 2, :]))

                def norm():
                    wait_own()
                    eng.wait_ge(s_st, k + 1)
                    eng.tensor_scalar(tt, tt, mv[0:n, k % 2, 0:1], rs[0:n, k % 2, :], ALU.subtract,
                                      ALU.mult).then_inc(s_dn, 1)

                ops = [first, mean0, mean1, mean2, residual]
                return ops if l < L - 1 else ops + [add_x, stats, aggr, recip, norm]

            steps = [0] * TB
            bases = {}
            def fast():
                for l in range(L):
                    todo = {}
                    for q in range(-6, ends[l]):
                        Q = l * NP + q
                        if 0 <= q < NP and q % 4 == 0:
                            w = min(8, NT - 2 * q)
                            _, vals = nc.values_load_multi_w_load_instructions(
                                brow[0:1, 2 * q:2 * q + w], engines=[DVE], min_val=0, max_val=R * (N - 1),
                                skip_runtime_bounds_check_because="three times a node's number")
                            bases.update({2 * q + i: v for i, v in enumerate(vals)})
                        if 0 <= q < NP and q % 2 == 0:
                            selectors(l, q)
                        if l == 0 and 0 <= q < NP:
                            for j in (2 * q, 2 * q + 1):
                                if j >= AR:
                                    eng.wait_ge(s_hc, j - AR + 1)
                                eng.tensor_scalar(oh_b[:, j % AR, :], iota[:, :], hb[:, j:j + 1], None,
                                                  ALU.is_equal).then_inc(s_ob, 1)
                        if l == 0 and (q + 6) // 2 < NG:
                            g, i = (q + 6) // 2, q % 2
                            eng.wait_ge(s_h[i], g + 1)
                            eng.tensor_tensor(an[:, g % 3, :, :], an[:, g % 3, :, :], hs[:, g % 2, :, 32 * i:32 * i + 32],
                                              ALU.subtract).then_inc(s_res, 1)
                        if 0 <= q < NP:
                            for i in range(2):
                                n = 2 * Q + i
                                eng.wait_ge(s_g[n % XR], 16 * (n // XR + 1))
                            eng.wait_ge(s_e, Q + 1)
                            v = xg[:, (2 * Q) % XR:(2 * Q) % XR + 2, :]
                            eng.tensor_tensor(v, v, pE[Q % 2][:, :].rearrange("p (i d) -> p i d", i=2),
                                              ALU.mult).then_inc(s_m, 1)
                        for k in list(todo):
                            todo[k].pop(0)()
                            if not todo[k]:
                                del todo[k]
                        for k in starting(l, q, 1):
                            todo[k] = block_ops(l, k)
                        if 0 <= q - 2 < NP:
                            V = Q - 2
                            if q == 2 and l:
                                eng.wait_ge(s_z, NB * l)
                            for i in range(2):
                                n = 2 * V + i
                                eng.wait_ge(s_sc, 2 * V + 2)
                                if n:
                                    eng.wait_ge(s_acc, n)
                                a = acc[:, :, bass.ds(bases.pop(2 * (q - 2) + i), WK)]
                                eng.tensor_tensor(a, a, pA[V % 2][:, 192 * i:192 * i + 192]
                                                  .rearrange("p (h w) -> p h w", h=2), ALU.add).then_inc(s_acc, 1)
                        if l == 0 and q == NP + 1:
                            eng.wait_ge(s_hc, NT)
                            eng.wait_ge(s_ob, NT)
                            eng.tensor_copy(cnt, pH[:, 0:147]).then_inc(s_cd, 1)
                            eng.wait_ge(s_cm, 1)
                            link(eng.tensor_scalar(inv[:, :], pH[:, 256:403], 1.0, None, ALU.max))
                            link(eng.reciprocal(inv[:, :], inv[:, :]))
                    assert not todo

            both(eng, "vector", fast)


_INS = ["x", "src", "dst", "edge_attr_32", "edge_type_3", "L0_gnn_weights", "L0_gnn_roots", "L0_gnn_biases",
        "L0_gnn_edge_w", "L0_gnn_edge_b"]


def kernel(**inputs):
    import numpy as _np
    import concourse.bacc as _bacc
    from concourse import mybir as _mybir
    from concourse.bass_utils import run_bass_kernel_spmd as _run

    nc = _bacc.Bacc("TRN2", target_bir_lowering=False, num_devices=1)
    arrays, args = {}, []
    for name in _INS:
        a = _np.ascontiguousarray(inputs[name])
        arrays[f"in_{name}_dram"] = a
        args.append(nc.dram_tensor(f"in_{name}_dram", a.shape, _mybir.dt.from_np(a.dtype), kind="ExternalInput").ap())
    due = block_limits()
    arrays["in_due_dram"] = due
    args.append(nc.dram_tensor("in_due_dram", due.shape, _mybir.dt.float32, kind="ExternalInput").ap())
    out = nc.dram_tensor("out_0_dram", (6250, 256), _mybir.dt.float32, kind="ExternalOutput").ap()
    gnn_program(nc, *args, out)
    r = _run(nc, [arrays], core_ids=[0])
    return r.results[0]["out_0_dram"]
```

```python
import concourse.bass as bass
from concourse import mybir
from contextlib import ExitStack


def block_starts():
    last, out = -4, []
    for k in range(49):
        tiles = min(782.0, 782.0 * (128 * (k + 1) / 6250.0) ** 0.5 + 6)
        q = max(int(tiles) // 2 + 4, last + 4)
        q += q % 2
        if k == 48:
            q = max(q, 394)
        out.append(q)
        last = q
    return out


def block_limits():
    import numpy as np

    limits = np.zeros(7 * 128, np.float32)
    for k, q in enumerate(block_starts()):
        j = min(782, 2 * (q - 2))
        limits[j:] = np.maximum(limits[j:], 128 * (k + 1))
    limits[782:] = 0
    return np.ascontiguousarray(limits.reshape(7, 128).T)


def gnn_program(nc, x_in, src, dst, edge_attr, edge_type, weights, roots, biases, edge_w, edge_b, due, out):
    F32, F32R, BF16, I32 = mybir.dt.float32, mybir.dt.float32r, mybir.dt.bfloat16, mybir.dt.int32
    ALU = mybir.AluOpType
    ACT = mybir.ActivationFunctionType
    AX = mybir.AxisListType
    DVE = mybir.EngineType.DVE

    N, E, D, R, L = 6250, 100000, 256, 3, 3
    NT = 782
    LAST = E - 128 * (NT - 1)
    NP = NT // 2
    CH = 7
    CL = NT - 128 * (CH - 1)
    WN = 32
    WK = WN * R
    ACC = N * R + WK
    NB = 49
    NLAST = N - 128 * (NB - 1)
    NG = NQ = 196
    XR, SR, TR, AR = 10, 8, 3, 4
    XB, XT, TB = 3, 2, 4
    PAD = 1000000
    BR = 448
    HIGH = -4096

    x1 = nc.dram_tensor("x1", (N, D), F32).ap()
    x2 = nc.dram_tensor("x2", (N, D), F32).ap()
    attr_t = nc.dram_tensor("attr_t", (NG, 64, 512), F32).ap()
    HR = 128 * R * NB
    sums = nc.dram_tensor("sums", (HR + 128, D), F32).ap()
    xs = [x_in, x1, x2, out]

    def rows(k):
        return 128 if k < NB - 1 else NLAST

    def tiles_of(g):
        return 4 if g < NG - 1 else NT - 4 * (NG - 1)

    def ring(l, i, depth, per):
        n = l * per + i
        return n % depth, n // depth + 1

    ctx = ExitStack()
    with ctx:
        def sb(name, shape, dt=F32):
            return ctx.enter_context(nc.sbuf_tensor(name, shape, dt))

        def sem(name):
            return ctx.enter_context(nc.semaphore(name))

        def sems(name, n):
            return [sem(f"{name}{i}") for i in range(n)]

        acc = sb("acc", [128, 2, ACC])
        accf = acc[:, :, :].rearrange("p h k -> p (h k)")
        idx = sb("idx", [128, NT], I32)
        kr = sb("kr", [128, NT], BF16)
        lo = sb("lo", [128, NT])
        hb = sb("hb", [128, NT])
        xg = sb("xg", [128, XR, D])
        S = sb("S", [128, SR, WK])
        at = sb("at", [128, TR, 512], F32R)
        hs = sb("hs", [128, 3, 4, 64])
        W = sb("W", [128, 8, D])
        bias = sb("bias", [128, D])
        wsb = sb("wsb", [128, 2, D], F32R)
        iota = sb("iota", [128, 148], BF16)
        ident = sb("ident", [128, 128])
        oh_a = sb("oh_a", [128, AR, 128], BF16)
        oh_b = sb("oh_b", [128, AR, 148], BF16)
        inv = sb("inv", [128, 147])
        cnt = sb("cnt", [128, 148])
        cd = sb("cd", [128, 2, 4])
        diff = sb("diff", [128, 128])
        brow = sb("brow", [33, BR], I32)
        base = sb("base", [128, CH])
        duet = sb("duet", [128, CH])
        bad = sb("bad", [128, 2])
        flag = sb("flag", [1, 1], I32)
        mask = sb("mask", [128, 1], I32)
        zcol = sb("zcol", [128, 1])
        ones = sb("ones", [128, 1])
        eps = sb("eps", [128, 1])
        xblk = sb("xblk", [128, XB, D])
        xT = sb("xT", [128, XT, D])
        t = sb("t", [128, TB, D])
        x0b = hb[:, 0:2 * D].rearrange("p (i d) -> p i d", i=2)
        bst = sb("bst", [128, 2, 6])
        mv = sb("mv", [128, 2, 2])
        sd = sb("sd", [128, 2, 1])
        rs = sb("rs", [128, 2, 1])
        nm = sb("nm", [128, 2, 1])

        P0 = 2 * ACC - 7 * 896 - D
        prep = [accf[:, P0 + 896 * i:P0 + 896 * (i + 1)] for i in range(7)]
        p_dst, p_typ, p_src = (p.bitcast(I32) for p in prep[0:3])
        p_f, p_rel, p_lo, p_hb = prep[3:7]
        p_high = p_f[:, 0:D]
        p_ew = accf[:, P0 + 7 * 896:P0 + 7 * 896 + D]

        def c3(p):
            return p.rearrange("q (c p) -> q c p", p=128)

        bank = [ctx.enter_context(nc.psum_tensor(f"bank{i}", [128, 512], F32)) for i in range(8)]
        pE = bank[0:2]
        pA = bank[2:4]
        pT = bank[4]
        pH = bank[5]
        pD = bank[6:8]

        s_pad, s_cst, s_id, s_zc, s_one, s_ez = (sem(n) for n in (
            "s_pad", "s_cst", "s_id", "s_zc", "s_one", "s_ez"))
        s_src, s_dst, s_typ, s_ew, s_due = (sem(n) for n in ("s_src", "s_dst", "s_typ", "s_eww", "s_due"))
        s_pf, s_pt, s_pc, s_idx, s_pca, s_wsb = (sem(n) for n in ("s_pf", "s_pt", "s_pc", "s_idx", "s_pca", "s_wsb"))
        s_ch = sem("s_ch")
        s_z0 = sem("s_z0")
        s_flag = sem("s_flag")
        s_g = sems("s_g", XR)
        s_e, s_m, s_r, s_S, s_sc, s_acc = (sem(n) for n in ("s_e", "s_m", "s_r", "s_S", "s_sc", "s_acc"))
        s_an = sems("s_an", 3)
        s_hi, s_lo, s_tr, s_atc = sem("s_hi"), sem("s_lo"), sem("s_tr"), sem("s_atc")
        s_ao = sems("s_ao", TR)
        s_at = sems("s_at", TR)
        s_oh, s_hc, s_cd, s_cm, s_inv, s_df = (sem(n) for n in (
            "s_oh", "s_hc", "s_cd", "s_cm", "s_inv", "s_df"))
        s_w = sem("s_w")
        s_xl = sems("s_xl", XB)
        s_x0 = sems("s_x0", 2)
        s_xt, s_xc, s_d0, s_d1, s_f0, s_f1, s_nm, s_z = (sem(n) for n in (
            "s_xt", "s_xc", "s_d0", "s_d1", "s_f0", "s_f1", "s_nm", "s_z"))
        s_rd, s_ax = sem("s_rd"), sem("s_ax")
        s_dc = sems("s_dc", TB)
        s_st, s_sq, s_no = sem("s_st"), sem("s_sq"), sem("s_no")
        s_xo = sems("s_xo", TB)

        producers = {"load": ("sync", 16), "swdge0": ("gpsimd", 16), "swdge1": ("gpsimd", 16),
                     "swdge2": ("gpsimd", 16), "pool": ("gpsimd", 1), "act": ("scalar", 1),
                     "pe": ("tensor", 1), "dve": ("vector", 1)}
        s_gen = {p: sem(f"s_gen_{p}") for p in producers}
        s_turn = {p: sem(f"s_turn_{p}") for p in ("sync", "gpsimd", "scalar", "tensor", "vector")}

        block = ctx.enter_context(nc.Block())

        def uses(l, i, depth, per):
            return len(range(i, l * per, depth))

        def starting(q, lag):
            return [k for k in range(NB) if starts[k] + lag == q]

        def acc_by(k):
            return min(NT, 2 * (starts[k] - 2))

        def slot(l, j):
            return 4 * ((l * NQ + j // 4) % (SR // 4)) + j % 4

        starts = block_starts()
        end = starts[-1] + 16

        G_x, G_sum = xg[:, 0, :], xg[:, 3, :]
        G_w, G_at = xg[0:33, 1, :], xg[0:33, 2, 0:128]
        G_eq, G_eqb, G_tri = xg[:, 4, 0:128], xg[:, 4, 128:256], xg[:, 5, 0:128]
        G_h = xg[:, 6:9, :]
        G_key, G_lo, G_hb, G_bef, G_ok, G_row, G_dump = (xg[:, 9, c:c + 1] for c in range(7))
        G_inv = xg[:, 9, 8:11]
        G_src, G_dst = (xg[:, 9, c:c + 1].bitcast(I32) for c in (12, 13))
        G_an = hs[:, 0, 0, 0:32]
        G_T = t[:, 0:4, :].rearrange("p a (b c) -> p (a b) c", c=128)
        G_t, G_x0, G_xb = xT[:, 0, :], xT[:, 1, :], xblk[:, 0, :]
        G_pk, G_pc = bank[0][:, 256:384], pH[:, 0:147]

        def start_steps():
            return [
                ("load", lambda e, i: e.dma_start(G_w[0:32, :], edge_w)),
                ("load", lambda e, i: e.dma_start(G_w[32:33, :], edge_b.rearrange("(a n) -> a n", a=1))),
                ("dve", lambda e, i: e.memset(G_at[32:33, :], 1.0)),
                ("dve", lambda e, i: e.memset(G_an, 0.0)),
                ("dve", lambda e, i: e.memset(inv[:, :], 0.0)),
                ("pool", lambda e, i: e.memset(G_tri, 1.0)),
                ("pool", lambda e, i: e.affine_select(out=G_tri, in_=G_tri, compare_op=ALU.is_gt, fill=0.0, base=0,
                                                      pattern=[[-1, 128]], channel_multiplier=1)),
                ("pool", lambda e, i: e.iota(G_dump, [[0, 1]], base=HR, channel_multiplier=1,
                                             allow_small_or_imprecise_dtypes=True)),
            ]

        def layer_steps(l):
            half = (HR + 128) // 2
            zero = [("load", lambda e, i, h=h: e.dma_start(
                sums[half * h:half * (h + 1), :].rearrange("(p r) d -> p (r d)", p=128),
                accf[:, 0:half * D // 128])) for h in range(2)]
            return zero + [("load", lambda e, i, r=r: e.dma_start(
                W[:, 2 * r:2 * r + 2, :],
                (weights[l, r] if r < R else roots[l]).rearrange("(h p) o -> p h o", p=128))) for r in range(R + 1)] + [
                ("load", lambda e, i: e.dma_start(bias[:, :], biases[l:l + 1, :].broadcast_to([128, D])))]

        def col(a, i):
            return a[:, i:i + 1] if isinstance(i, int) else a[:, bass.ds(i, 1)]

        def edge_steps(l, n):
            steps = [
                ("load", lambda e, i: e.dma_start(G_an[0:n, :], edge_attr[bass.ds(i * 128, n), :])),
                ("pe", lambda e, i: e.transpose(pT[0:32, 0:128], G_an, ident[:, :])),
                ("act", lambda e, i: e.activation(G_at[0:32, :], pT[0:32, 0:128], ACT.Copy)),
                ("pe", lambda e, i: e.matmul(pE[0][:, 0:256], G_at, G_w, start=True, stop=True)),
                ("dve", lambda e, i: e.tensor_copy(G_src, col(idx, i))),
                ("dve", lambda e, i: e.tensor_copy(G_lo, col(lo, i))),
                ("dve", lambda e, i: e.tensor_copy(G_hb, col(hb, i))),
                (f"swdge{l}", lambda e, i: e.indirect_dma_start(
                    out=G_x, out_offset=None, in_=xs[l],
                    in_offset=bass.IndirectOffsetOnAxis(ap=G_src, axis=0))),
                ("dve", lambda e, i: e.tensor_tensor(G_x, G_x, pE[0][:, 0:256], ALU.mult)),
                ("act", lambda e, i: e.activation(G_x, G_x, ACT.Relu)),
                ("dve", lambda e, i: e.scalar_tensor_tensor(G_key, G_hb, -128.0, G_lo, ALU.mult, ALU.subtract)),
                ("dve", lambda e, i: e.tensor_scalar(G_key, G_key, 64.5, None, ALU.add)),
                ("pe", lambda e, i: e.matmul(G_pk, G_key.to_broadcast([128, 128]), ident[:, :],
                                             start=True, stop=True)),
                ("dve", lambda e, i: e.tensor_scalar(G_eq, G_pk, G_key, None, ALU.is_equal)),
                ("dve", lambda e, i: e.tensor_tensor(G_eqb, G_eq, G_tri, ALU.mult)),
                ("dve", lambda e, i: e.tensor_reduce(G_bef, G_eqb, AX.X, ALU.add)),
                ("dve", lambda e, i: e.tensor_scalar(G_ok, G_key, float(HR), None, ALU.is_lt)),
                ("dve", lambda e, i: e.scalar_tensor_tensor(G_ok, G_bef, 0.5, G_ok, ALU.is_lt, ALU.mult)),
                ("dve", lambda e, i: e.tensor_tensor(G_row, G_key, G_dump, ALU.subtract)),
                ("dve", lambda e, i: e.tensor_tensor(G_row, G_row, G_ok, ALU.mult)),
                ("dve", lambda e, i: e.tensor_tensor(G_row, G_row, G_dump, ALU.add)),
                ("dve", lambda e, i: e.tensor_copy(G_dst, G_row)),
                ("pe", lambda e, i: e.matmul(pA[0][:, 0:256], G_eq, G_x, start=True, stop=True)),
                ("act", lambda e, i: e.activation(G_sum, pA[0][:, 0:256], ACT.Copy)),
                (f"swdge{l}", lambda e, i: e.indirect_dma_start(
                    out=sums, out_offset=bass.IndirectOffsetOnAxis(ap=G_dst, axis=0), in_=G_sum, in_offset=None,
                    compute_op=ALU.add, oob_is_err=True)),
            ]
            if l == 0:
                steps += [
                    ("dve", lambda e, i: e.tensor_scalar(oh_a[:, 0, :], iota[:, 1:129], G_lo, 0.5, ALU.add,
                                                         ALU.is_equal)),
                    ("dve", lambda e, i: e.tensor_scalar(oh_b[:, 0, 0:147], iota[:, 1:148], G_hb, 0.5, ALU.add,
                                                         ALU.is_equal)),
                    ("pe", lambda e, i: e.matmul(G_pc, oh_a[:, 0, :], oh_b[:, 0, 0:147], start=True, stop=True)),
                    ("dve", lambda e, i: e.tensor_tensor(inv[:, :], inv[:, :], G_pc, ALU.add)),
                ]
            return steps

        def count_steps():
            return [
                ("dve", lambda e, i: e.tensor_scalar(inv[:, :], inv[:, :], 1.0, None, ALU.max)),
                ("dve", lambda e, i: e.reciprocal(inv[:, :], inv[:, :])),
            ]

        def turn_all(e, n):
            for h in range(2):
                e.transpose(bank[0][:, 128 * h:128 * h + n], G_xb[0:n, 128 * h:128 * h + 128], ident[0:n, 0:n])
            for m in range(2, 8):
                ins = e.transpose(bank[m // 4][:, 128 * (m % 4):128 * (m % 4) + 128],
                                  G_h[:, m // 2 - 1, 128 * (m % 2):128 * (m % 2) + 128], ident[:, :])
            return ins

        def mix_all(e, n):
            for m in range(4):
                for h in range(2):
                    ins = e.matmul(pD[m // 2][0:n, 256 * (m % 2):256 * (m % 2) + 256], G_T[:, 2 * m + h, 0:n],
                                   W[:, 2 * ((m - 1) % 4) + h, :], start=(h == 0), stop=(h == 1))
            return ins

        def node_steps(l, n):
            tt = G_t[0:n, :]
            steps = [
                ("load", lambda e, i: e.dma_start(G_h, sums[bass.ds(i * (3 * 128), 3 * 128), :]
                                                  .rearrange("(r p) d -> p r d", p=128))),
                ("load", lambda e, i: e.dma_start(G_xb[0:n, :], xs[l][bass.ds(i * 128, n), :])),
                ("pe", lambda e, i: turn_all(e, n)),
                ("act", lambda e, i: e.activation(G_T[:, 0:2, 0:n], bank[0][:, 0:256]
                                                  .rearrange("p (a c) -> p a c", c=128)[:, :, 0:n], ACT.Copy)),
                ("act", lambda e, i: e.activation(G_T[:, 2:4, :], bank[0][:, 256:512]
                                                  .rearrange("p (a c) -> p a c", c=128), ACT.Copy)),
                ("act", lambda e, i: e.activation(G_T[:, 4:8, :], bank[1][:, :]
                                                  .rearrange("p (a c) -> p a c", c=128), ACT.Copy)),
                ("pe", lambda e, i: mix_all(e, n)),
                ("dve", lambda e, i: e.tensor_copy(G_inv, inv[:, bass.ds(i * 3, 3)])),
                ("dve", lambda e, i: e.tensor_tensor(tt, pD[0][0:n, 0:256], bias[0:n, :], ALU.add)),
            ] + [
                ("dve", lambda e, i, m=m: e.scalar_tensor_tensor(
                    tt, pD[m // 2][0:n, 256 * (m % 2):256 * (m % 2) + 256], G_inv[0:n, m - 1:m], tt,
                    ALU.mult, ALU.add)) for m in (1, 2, 3)
            ] + [
                ("dve", lambda e, i: e.scalar_tensor_tensor(tt, tt, 0.0, G_xb[0:n, :], ALU.max, ALU.add)),
            ]
            if l == L - 1:
                b, m, d, r = bst[0:n, 0, :], mv[0:n, 0, :], sd[0:n, 0, :], rs[0:n, 0, :]
                steps += [
                    ("load", lambda e, i: e.dma_start(G_x0[0:n, :], x_in[bass.ds(i * 128, n), :])),
                    ("dve", lambda e, i: e.tensor_tensor(tt, tt, G_x0[0:n, :], ALU.add)),
                    ("dve", lambda e, i: e.bn_stats(b, tt)),
                    ("dve", lambda e, i: e.bn_aggr(m, b)),
                    ("act", lambda e, i: e.activation(d, m[:, 1:2], ACT.Sqrt, bias=eps[0:n, :])),
                    ("dve", lambda e, i: e.reciprocal(r, d)),
                    ("dve", lambda e, i: e.tensor_scalar(tt, tt, m[:, 0:1], r, ALU.subtract, ALU.mult)),
                ]
            return steps + [("load", lambda e, i: e.dma_start(xs[l + 1][bass.ds(i * 128, n), :], tt))]

        def general(eng, name):
            done = dict.fromkeys(producers, 0)
            last = [None]

            def phase(steps, i0=0, times=1):
                per = {p: producers[p][1] * sum(s[0] == p for s in steps) for p in producers}

                def issue(i, turn):
                    now = dict(done)
                    prev = (steps[-1][0], now[steps[-1][0]] + turn * per[steps[-1][0]])
                    for p, step in steps:
                        now[p] += producers[p][1]
                        if producers[p][0] == name:
                            eng.wait_ge(s_gen[prev[0]], prev[1])
                            eng.sem_inc(s_turn[name], 1)
                            step(eng, i).then_inc(s_gen[p], producers[p][1])
                        prev = (p, now[p] + turn * per[p])

                mine = any(producers[p][0] == name for p, _ in steps)
                if producers[steps[0][0]][0] == name and last[0]:
                    eng.wait_ge(s_gen[last[0]], done[last[0]])
                if mine and times == 1:
                    issue(i0, 0)
                elif mine:
                    with eng.Fori(i0, i0 + times) as i:
                        issue(i, i - i0)
                for p in producers:
                    done[p] += times * per[p]
                last[0] = steps[-1][0]

            phase(start_steps())
            for l in range(L):
                phase(layer_steps(l))
                phase(edge_steps(l, 128))
                phase(edge_steps(l, 128), 1, NT - 2)
                phase(edge_steps(l, LAST), NT - 1)
                if l == 0:
                    phase(count_steps())
                phase(node_steps(l, 128), 0, NB - 1)
                phase(node_steps(l, NLAST), NB - 1)
            if name == "sync":
                eng.wait_ge(s_gen["load"], done["load"])
                for l in range(L):
                    eng.wait_ge(s_gen[f"swdge{l}"], done[f"swdge{l}"])

        def both(eng, name, fast):
            eng.wait_ge(s_flag, 4)
            late = eng.value_load(flag[0:1, 0:1], min_val=0, max_val=128 * 128 * CH + 128 * CH)
            with eng.If(late == 0):
                fast()
            with eng.Else():
                general(eng, name)

        @block.sync
        def _(eng):
            eng.wait_ge(s_pad, 3)
            for p, a, s in ((p_src, src, s_src), (p_dst, dst, s_dst), (p_typ, edge_type, s_typ)):
                eng.dma_start(c3(p)[:, 0:CH - 1, :],
                              a[0:128 * 128 * (CH - 1)].rearrange("(c q p) -> q c p", q=128, p=128)).then_inc(s, 16)
                eng.dma_start(c3(p)[0:CL - 1, CH - 1, :],
                              a[128 * 128 * (CH - 1):128 * (NT - 1)].rearrange("(q p) -> q p", p=128)).then_inc(s, 16)
                eng.dma_start(c3(p)[CL - 1:CL, CH - 1, 0:LAST],
                              a[128 * (NT - 1):E].rearrange("(q p) -> q p", q=1)).then_inc(s, 16)
            eng.wait_ge(s_ez, 1)
            for i in range(2):
                eng.dma_start(p_ew[32 * i:32 * i + 32, :], edge_w).then_inc(s_ew, 16)
            eng.dma_start(p_ew[64:65, :], edge_b.rearrange("(a n) -> a n", a=1)).then_inc(s_ew, 16)
            eng.dma_start(duet[:, :], due).then_inc(s_due, 16)

            def load_weights(l):
                if l:
                    eng.wait_ge(s_rd, NB * l)
                for i in range(R):
                    eng.dma_start(W[:, 2 * i:2 * i + 2, :],
                                  weights[l, i].rearrange("(h p) o -> p h o", p=128)).then_inc(s_w, 16)
                eng.dma_start(W[:, 6:8, :], roots[l].rearrange("(h p) o -> p h o", p=128)).then_inc(s_w, 16)
                eng.dma_start(bias[:, :], biases[l:l + 1, :].broadcast_to([128, D])).then_inc(s_w, 16)

            def load_attr(g):
                if g >= 3:
                    eng.wait_ge(s_tr, g - 2)
                if g < NG - 1:
                    eng.dma_start(hs[:, g % 3, :, 32:64], edge_attr[512 * g:512 * (g + 1), :]
                                  .rearrange("(j p) d -> p j d", p=128)).then_inc(s_an[g % 3], 16)
                else:
                    eng.dma_start(hs[:, g % 3, 0, 32:64], edge_attr[512 * g:512 * g + 128, :]).then_inc(s_an[g % 3], 16)
                    eng.dma_start(hs[0:LAST, g % 3, 1, 32:64], edge_attr[128 * (NT - 1):E, :]).then_inc(s_an[g % 3], 16)

            def keep_attr(g):
                w = 128 * tiles_of(g)
                eng.wait_ge(s_atc, g + 1)
                eng.dma_start(attr_t[g, :, 0:w], at[0:64, g % TR, 0:w].bitcast(F32)).then_inc(s_ao[g % TR], 16)

            def reload_attr(l, g):
                G = l * NG + g
                eng.wait_ge(s_e, l * NP + 2 * max(0, g - TR + 1))
                w = 128 * tiles_of(g)
                eng.dma_start(at[0:64, G % TR, 0:w].bitcast(F32), attr_t[g, :, 0:w]).then_inc(s_at[G % TR], 16)

            def load_x(l, k):
                K, n = NB * l + k, rows(k)
                if K >= XB:
                    eng.wait_ge(s_rd, K - XB + 1)
                eng.dma_start(xblk[0:n, K % XB, :], xs[l][128 * k:128 * k + n, :]).then_inc(s_xl[K % XB], 16)

            def load_x0(k):
                n = rows(k)
                if k >= 2:
                    eng.wait_ge(s_ax, k - 1)
                eng.dma_start(x0b[0:n, k % 2, :], x_in[128 * k:128 * k + n, :]).then_inc(s_x0[k % 2], 16)

            def store(l, k):
                K, n = NB * l + k, rows(k)
                if l < L - 1:
                    eng.wait_ge(s_rd, K + 1)
                else:
                    eng.wait_ge(s_no, k + 1)
                eng.dma_start(xs[l + 1][128 * k:128 * k + n, :], t[0:n, K % TB, :]).then_inc(s_xo[K % TB], 16)

            def fast():
                for g in range(3):
                    load_attr(g)
                for l in range(L):
                    late = 9 if l < L - 1 else 15
                    for q in range(-4, end):
                        if l == 0 and q % 2 == 0:
                            if 3 <= q // 2 + 4 < NG:
                                load_attr(q // 2 + 4)
                            if 0 <= q // 2 < NG:
                                keep_attr(q // 2)
                        if l and q % 2 == 0 and q // 2 + 2 < NG:
                            reload_attr(l, q // 2 + 2)
                        if q == 0:
                            for i in range(TB if l else 0):
                                eng.wait_ge(s_xo[i], 16 * uses(l, i, TB, NB))
                            load_weights(l)
                            for k in range(XB):
                                load_x(l, k)
                            if l == L - 1:
                                load_x0(0)
                                load_x0(1)
                        for k in starting(q, 8):
                            if k + XB < NB:
                                load_x(l, k + XB)
                        for k in starting(q, 9):
                            if l == L - 1 and k + 2 < NB:
                                load_x0(k + 2)
                        for k in starting(q, late):
                            store(l, k)
                    if l == 0:
                        for i in range(TR):
                            eng.wait_ge(s_ao[i], 16 * uses(1, i, TR, NG))
                for i in range(TB):
                    eng.wait_ge(s_xo[i], 16 * uses(L, i, TB, NB))

            both(eng, "sync", fast)

        @block.gpsimd
        def _(eng):
            eng.memset(c3(p_src)[:, CH - 1, :], 0).then_inc(s_pad, 1)
            eng.memset(c3(p_dst)[:, CH - 1, :], PAD).then_inc(s_pad, 1)
            eng.memset(c3(p_typ)[:, CH - 1, :], 0).then_inc(s_pad, 1)
            eng.memset(zcol[:, :], 0.0).then_inc(s_zc, 1)
            eng.memset(p_ew, 0.0).then_inc(s_ez, 1)
            eng.memset(ident[:, :], 0.0).then_inc(s_id, 1)
            eng.wait_ge(s_id, 1)
            eng.affine_select(out=ident[:, :], in_=ident[:, :], compare_op=ALU.not_equal, fill=1.0,
                              base=0, pattern=[[-1, 128]], channel_multiplier=1).then_inc(s_id, 1)
            eng.iota(iota[:, :], [[1, 148]], base=-1, channel_multiplier=0,
                     allow_small_or_imprecise_dtypes=True).then_inc(s_cst, 1)
            eng.memset(ones[:, :], 1.0).then_inc(s_cst, 1)
            eng.memset(mask[:, :], HIGH).then_inc(s_cst, 1)
            eng.memset(eps[:, :], 1e-5).then_inc(s_cst, 1)
            eng.memset(accf[:, 24000:P0], 0.0).then_inc(s_z0, 1)
            eng.memset(diff[:, :], 0.0).then_inc(s_df, 1)
            for i, (fill, b) in enumerate(((0.25, 0), (-0.25, 1), (0.25, -127))):
                eng.wait_ge(s_df, i + 1)
                eng.affine_select(out=diff[:, :], in_=diff[:, :], compare_op=ALU.not_equal, fill=fill,
                                  base=b, pattern=[[-1, 128]], channel_multiplier=1).then_inc(s_df, 1)
            eng.wait_ge(s_idx, 2)
            def fast():
                for l in range(L):
                    if l:
                        for i in range(TB):
                            eng.wait_ge(s_xo[i], 16 * uses(l, i, TB, NB))
                    for j in range(NT):
                        n = l * NT + j
                        if n >= XR:
                            eng.wait_ge(s_sc, 2 * ((n - XR) // 2 + 1))
                        eng.indirect_dma_start(
                            out=xg[:, n % XR, :], out_offset=None, in_=xs[l],
                            in_offset=bass.IndirectOffsetOnAxis(ap=idx[:, j:j + 1], axis=0)).then_inc(s_g[n % XR], 16)

            both(eng, "gpsimd", fast)

        @block.scalar
        def _(eng):
            eng.wait_ge(s_zc, 1)
            for a in range(0, 24000, 6000):
                eng.activation(accf[:, a:a + 6000], zcol[:, 0:1].to_broadcast([128, 6000]), ACT.Copy).then_inc(s_z0, 1)

            def copies(dstn, b0, b1):
                eng.activation(dstn[:, 0:512], b0[:, 0:512], ACT.Copy).then_inc(s_pca, 1)
                eng.activation(dstn[:, 512:NT], b1[:, 0:NT - 512], ACT.Copy).then_inc(s_pca, 1)

            eng.wait_ge(s_pt, 3)
            copies(lo, bank[4], bank[5])
            eng.wait_ge(s_pt, 4)
            copies(hb, bank[6], bank[7])

            def attr_copy(g):
                w = 128 * tiles_of(g)
                eng.wait_ge(s_tr, g + 1)
                if g >= TR:
                    eng.wait_ge(s_e, 2 * (g - TR + 1))
                    eng.wait_ge(s_ao[g % TR], 16 * (g // TR))
                eng.activation(at[0:64, g % TR, 0:w], pT[0:64, 0:w], ACT.Copy).then_inc(s_atc, 1)

            def root(k):
                par, n = k % 2, rows(k)
                eng.wait_ge(s_st, k + 1)
                eng.activation(sd[0:n, par, :], mv[0:n, par, 1:2], ACT.Sqrt, bias=eps[0:n, :]).then_inc(s_sq, 1)

            def norm(k):
                K, par, n = NB * (L - 1) + k, k % 2, rows(k)
                eng.wait_ge(s_nm, k + 1)
                eng.activation(t[0:n, K % TB, :], t[0:n, K % TB, :], ACT.Identity, scale=rs[0:n, par, :],
                               bias=nm[0:n, par, :]).then_inc(s_no, 1)

            def fast():
                for l in range(L):
                    for q in range(-6, end):
                        Q = l * NP + q
                        if 0 <= q < NP:
                            eng.wait_ge(s_m, Q + 1)
                            v = xg[:, (2 * Q) % XR:(2 * Q) % XR + 2, :]
                            eng.activation(v, v, ACT.Relu).then_inc(s_r, 1)
                        if l == 0 and q % 2 == 0 and (q + 2) // 2 < NG:
                            if q >= -2:
                                attr_copy((q + 2) // 2)
                        for k in starting(q, -1):
                            K, n = NB * l + k, rows(k)
                            eng.wait_ge(s_xt, K + 1)
                            if K >= XT:
                                eng.wait_ge(s_d0, K - XT + 1)
                            eng.activation(xT[:, K % XT, :].rearrange("p (h n) -> p h n", h=2)[:, :, 0:n],
                                           pT[:, 0:256].rearrange("p (h n) -> p h n", h=2)[:, :, 0:n],
                                           ACT.Copy).then_inc(s_xc, 1)
                        if l == 0 and 0 <= q < NP:
                            for j in (2 * q, 2 * q + 1):
                                if j >= AR:
                                    eng.wait_ge(s_hc, j - AR + 1)
                                eng.activation(oh_a[:, j % AR, :], iota[:, 1:129], ACT.Sign, bias=lo[:, j:j + 1])
                                eng.activation(oh_b[:, j % AR, :], iota[:, :], ACT.Sign,
                                               bias=hb[:, j:j + 1]).then_inc(s_oh, 1)
                        if l < L - 1:
                            for k in starting(q, 5):
                                eng.wait_ge(s_d1, NB * l + k + 1)
                                b = 384 * (k + 1) if k < NB - 1 else ACC
                                eng.activation(acc[:, :, 384 * k:b], zcol[:, 0:1].unsqueeze(2)
                                               .to_broadcast([128, 2, b - 384 * k]), ACT.Copy).then_inc(s_z, 1)
                        else:
                            for k in starting(q, 11):
                                root(k)
                            for k in starting(q, 14):
                                norm(k)

            both(eng, "scalar", fast)

        @block.tensor
        def _(eng):
            eng.wait_ge(s_id, 2)

            def turn(p, b0, b1):
                for c in range(CH):
                    q = 128 if c < CH - 1 else CL
                    b = b0 if c < 4 else b1
                    last = eng.transpose(b[:, 128 * (c % 4):128 * (c % 4) + q], c3(p)[0:q, c, :], ident[0:q, 0:q])
                last.then_inc(s_pt, 1)

            eng.wait_ge(s_pf, 1)
            turn(p_f, bank[0], bank[1])
            eng.wait_ge(s_pf, 2)
            turn(p_rel, bank[2], bank[3])
            eng.wait_ge(s_pf, 3)
            turn(p_lo, bank[4], bank[5])
            eng.wait_ge(s_pf, 4)
            turn(p_hb, bank[6], bank[7])
            eng.wait_ge(s_idx, 2)
            eng.wait_ge(s_pf, 5)
            eng.wait_ge(s_cst, 2)
            for c in range(CH):
                eng.matmul(bank[c // 4][0:1, 128 * (c % 4):128 * (c % 4) + 128], base[:, c:c + 1], ident[:, :],
                           start=True, stop=True)
            eng.matmul(bank[1][0:1, 510:511], bad[:, 0:1], ones[:, :], start=True, stop=False)
            eng.matmul(bank[1][0:1, 510:511], bad[:, 1:2], ones[:, :], start=False, stop=True).then_inc(s_pt, 1)
            eng.wait_ge(s_flag, 4)
            eng.wait_ge(s_pc, 2)
            eng.wait_ge(s_pca, 4)
            eng.wait_ge(s_wsb, 2)
            eng.wait_ge(s_one, 1)

            def attr_turn(g):
                eng.wait_ge(s_lo, g + 1)
                eng.wait_ge(s_atc, g)
                eng.wait_ge(s_xc, turned[0])
                for i in range(tiles_of(g)):
                    last = eng.transpose(pT[0:64, 128 * i:128 * i + 128], hs[:, g % 3, i, :], ident[:, :])
                last.then_inc(s_tr, 1)

            def edge_weights(l, q):
                Q = l * NP + q
                g = q // 2
                sl, times = ring(l, g, TR, NG)
                if q % 2 == 0:
                    if l == 0:
                        eng.wait_ge(s_atc, g + 1)
                    else:
                        eng.wait_ge(s_at[sl], 16 * (times - uses(1, sl, TR, NG)))
                if Q >= 2:
                    eng.wait_ge(s_m, Q - 1)
                for i in range(2):
                    c = 256 * (q % 2) + 128 * i
                    for p in range(2):
                        last = eng.matmul(pE[Q % 2][:, 256 * i:256 * i + 256], at[:, sl, c:c + 128],
                                          wsb[:, p, :], start=(p == 0), stop=(p == 1))
                last.then_inc(s_e, 1)

            def collect(l, q):
                V = l * NP + q
                eng.wait_ge(s_r, V + 1)
                if V >= 2:
                    eng.wait_ge(s_acc, 2 * (V - 1))
                eng.wait_ge(s_S, q // 2 + 1 + l * NQ)
                for i in range(2):
                    n = 2 * V + i
                    for h in range(2):
                        last = eng.matmul(pA[V % 2][:, 192 * i + 96 * h:192 * i + 96 * h + 96],
                                          xg[:, n % XR, 128 * h:128 * h + 128], S[:, slot(l, 2 * q + i), :],
                                          start=True, stop=True)
                    last.then_inc(s_sc, 1)

            def histogram(q):
                eng.wait_ge(s_cd, sum(acc_by(k) <= 2 * q for k in range(NB)))
                for n in (2 * q, 2 * q + 1):
                    eng.wait_ge(s_oh, n + 1)
                    eng.matmul(pH[:, 0:148], oh_a[:, n % AR, :], oh_b[:, n % AR, :], start=(n in cuts),
                               stop=(n + 1 in cuts)).then_inc(s_hc, 1)

            def count(k):
                V = starts[k]
                if k == 0:
                    eng.wait_ge(s_df, 4)
                eng.wait_ge(s_cd, k + 1)
                eng.wait_ge(s_acc, min(NT, 2 * (V - 1)))
                eng.matmul(pA[V % 2][:, 384:388], diff[:, :], cnt[:, 3 * k:3 * k + 4], start=True, stop=True).then_inc(s_cm, 1)

            def turn_x(l, k):
                K, n = NB * l + k, rows(k)
                eng.wait_ge(s_xl[K % XB], 16 * (K // XB + 1))
                if K:
                    eng.wait_ge(s_xc, K)
                if l == 0:
                    eng.wait_ge(s_atc, min(NG, starts[k] // 2 + 1))
                    turned[0] += 1
                for h in range(2):
                    last = eng.transpose(pT[:, 128 * h:128 * h + n], xblk[0:n, K % XB, 128 * h:128 * h + 128],
                                         ident[0:n, 0:n])
                last.then_inc(s_xt, 1)

            def mix(l, k, m):
                K, n = NB * l + k, rows(k)
                o = pD[m // 2][0:n, 256 * (m % 2):256 * (m % 2) + 256]
                if m == 0:
                    eng.wait_ge(s_xc, K + 1)
                    eng.wait_ge(s_f0, K)
                    if k == 0:
                        eng.wait_ge(s_w, 80 * (l + 1))
                if m == 1:
                    eng.wait_ge(s_acc, l * NT + acc_by(k))
                if m == 2:
                    eng.wait_ge(s_f1, K)
                for h in range(2):
                    r = m - 1
                    a = (acc[:, h, 384 * k + r:384 * k + r + 3 * (n - 1) + 1:3] if m
                         else xT[:, K % XT, 128 * h:128 * h + n])
                    last = eng.matmul(o, a, W[:, 2 * (r % 4) + h, :], start=(h == 0), stop=(h == 1))
                if m % 2:
                    last.then_inc(pair_done[m // 2], 1)

            cuts = [0] + [acc_by(k) for k in range(NB)]
            pair_done = [s_d0, s_d1]
            turned = [0]
            def fast():
                for l in range(L):
                    for q in range(-3, end):
                        if l == 0 and 0 <= q - 2 < NP:
                            histogram(q - 2)
                        for m in range(R + 1):
                            for k in starting(q, 1 + m):
                                mix(l, k, m)
                        if 0 <= q + 1 < NP:
                            edge_weights(l, q + 1)
                        if l == 0:
                            for k in starting(q, 1):
                                count(k)
                        if 0 <= q - 1 < NP:
                            collect(l, q - 1)
                        if l == 0 and q % 2 and (q + 3) // 2 < NG:
                            attr_turn((q + 3) // 2)
                        for k in starting(q, -2):
                            turn_x(l, k)

            both(eng, "tensor", fast)

        @block.vector
        def _(eng):
            chain = [0]

            def link(ins):
                chain[0] += 1
                ins.then_inc(s_ch, 1)
                eng.wait_ge(s_ch, chain[0])

            eng.memset(at[64:128, :, :].bitcast(F32), 1.0).then_inc(s_one, 1)
            eng.wait_ge(s_src, 48)
            eng.tensor_copy(p_f, p_src).then_inc(s_pf, 1)
            eng.wait_ge(s_pt, 1)
            eng.tensor_copy(idx[:, 0:512], bank[0][:, 0:512]).then_inc(s_idx, 1)
            eng.tensor_copy(idx[:, 512:NT], bank[1][:, 0:NT - 512]).then_inc(s_idx, 1)
            eng.wait_ge(s_dst, 48)
            eng.wait_ge(s_typ, 48)
            link(eng.tensor_copy(p_f, p_dst))
            link(eng.tensor_reduce(base[:, :], c3(p_f), AX.X, ALU.min))
            link(eng.tensor_tensor(c3(p_lo), c3(p_f), base[:, :].unsqueeze(2).to_broadcast([128, CH, 128]),
                                   ALU.subtract))
            link(eng.scalar_tensor_tensor(p_rel, p_lo, 3.0, p_typ, ALU.mult, ALU.add))
            eng.sem_inc(s_pf, 1)
            link(eng.tensor_scalar(p_hb, p_lo, float(PAD) / 2, None, ALU.is_lt))
            link(eng.scalar_tensor_tensor(p_hb, p_lo, float(WN), p_hb, ALU.is_ge, ALU.mult))
            link(eng.tensor_reduce(bad[:, 0:1], p_hb, AX.X, ALU.add))
            eng.wait_ge(s_due, 16)
            link(eng.tensor_tensor(duet[:, :], base[:, :], duet[:, :], ALU.is_lt))
            link(eng.tensor_reduce(bad[:, 1:2], duet[:, :], AX.X, ALU.add))
            link(eng.tensor_scalar(p_src, p_dst, 127, None, ALU.bitwise_and))
            link(eng.tensor_scalar(p_lo, p_src, -1.0, 0.5, ALU.mult, ALU.add))
            eng.sem_inc(s_pf, 1)
            link(eng.tensor_scalar(p_src, p_dst, 7, None, ALU.logical_shift_right))
            link(eng.scalar_tensor_tensor(p_hb, p_src, -3.0, p_typ, ALU.mult, ALU.subtract))
            link(eng.tensor_scalar(p_hb, p_hb, 0.5, None, ALU.add))
            eng.sem_inc(s_pf, 1)
            eng.sem_inc(s_pf, 1)
            eng.wait_ge(s_ew, 48)
            eng.wait_ge(s_cst, 3)
            link(eng.tensor_tensor(p_high.bitcast(I32), p_ew.bitcast(I32), mask[:, :].to_broadcast([128, D]),
                                   ALU.bitwise_and))
            eng.tensor_copy(wsb[:, 0, :], p_high).then_inc(s_wsb, 1)
            eng.tensor_tensor(wsb[:, 1, :], p_ew, p_high, ALU.subtract).then_inc(s_wsb, 1)
            eng.wait_ge(s_pt, 2)
            eng.tensor_copy(kr[:, 0:512], bank[2][:, 0:512]).then_inc(s_pc, 1)
            eng.tensor_copy(kr[:, 512:NT], bank[3][:, 0:NT - 512]).then_inc(s_pc, 1)
            eng.wait_ge(s_pt, 5)
            for a, b in ((brow[0:1, 0:BR], bank[0][0:1, 0:BR]),
                         (brow[32:33, 0:512 - BR], bank[0][0:1, BR:512]),
                         (brow[32:33, 512 - BR:BR], bank[1][0:1, 0:384])):
                eng.tensor_scalar(a, b, 3.0, None, ALU.mult).then_inc(s_flag, 1)
            eng.tensor_copy(flag[:, :], bank[1][0:1, 510:511]).then_inc(s_flag, 1)
            eng.wait_ge(s_wsb, 2)
            link(eng.memset(accf[:, P0:2 * ACC], 0.0))
            eng.wait_ge(s_z0, 5)
            eng.wait_ge(s_cst, 4)
            eng.wait_ge(s_pca, 4)
            eng.wait_ge(s_flag, 4)
            eng.wait_ge(s_pc, 2)

            def selectors(l, q):
                j, w = 2 * q, min(4, NT - 2 * q)
                at4 = slot(l, j)
                if l or j >= SR:
                    eng.wait_ge(s_sc, l * NT + (j - 4 if j >= SR else 0 if j else -2))
                eng.tensor_tensor(S[:, at4:at4 + w, :], iota[:, 1:WK + 1].unsqueeze(1).to_broadcast([128, w, WK]),
                                  kr[:, j:j + w].unsqueeze(2).to_broadcast([128, w, WK]),
                                  ALU.is_equal).then_inc(s_S, 1)

            def split(g, i):
                raw, high = hs[:, g % 3, :, 32:64], hs[:, g % 3, :, 0:32]
                if i == 0:
                    eng.wait_ge(s_an[g % 3], 16 * (g // 3 + 1) + (16 if g == NG - 1 else 0))
                    eng.tensor_tensor(high.bitcast(I32), raw.bitcast(I32),
                                      mask[:, :].unsqueeze(2).to_broadcast([128, 4, 32]),
                                      ALU.bitwise_and).then_inc(s_hi, 1)
                else:
                    eng.wait_ge(s_hi, g + 1)
                    eng.tensor_tensor(raw, raw, high, ALU.subtract).then_inc(s_lo, 1)

            def add_sums(l, q, i):
                V = l * NP + q
                n = 2 * V + i
                eng.wait_ge(s_sc, 2 * V + 2)
                if n:
                    eng.wait_ge(s_acc, n)
                a = acc[:, :, bass.ds(bases.pop(2 * q + i), WK)]
                eng.tensor_tensor(a, a, pA[V % 2][:, 192 * i:192 * i + 192]
                                  .rearrange("p (h w) -> p h w", h=2), ALU.add).then_inc(s_acc, 1)

            def block_ops(l, k):
                K, n = NB * l + k, rows(k)
                i = K % TB
                tt = t[0:n, i, :]

                def wait_own():
                    eng.wait_ge(s_dc[i], steps[i])

                def op(ins):
                    steps[i] += 1
                    ins.then_inc(s_dc[i], 1)

                def mean(r):
                    m = r + 1
                    return eng.scalar_tensor_tensor(tt, pD[m // 2][0:n, 256 * (m % 2):256 * (m % 2) + 256],
                                                    inv[0:n, 3 * k + r:3 * k + r + 1], tt, ALU.mult, ALU.add)

                def first():
                    eng.wait_ge(s_d0, K + 1)
                    eng.wait_ge(s_xo[i], 16 * (K // TB))
                    op(eng.tensor_tensor(tt, pD[0][0:n, 0:256], bias[0:n, :], ALU.add))

                def mean0():
                    wait_own()
                    eng.wait_ge(s_inv, 4 * min(K + 1, NB))
                    mean(0).then_inc(s_f0, 1)

                def mean1():
                    eng.wait_ge(s_f0, K + 1)
                    eng.wait_ge(s_d1, K + 1)
                    op(mean(1))

                def mean2():
                    wait_own()
                    mean(2).then_inc(s_f1, 1)

                def residual():
                    eng.wait_ge(s_f1, K + 1)
                    eng.scalar_tensor_tensor(tt, tt, 0.0, xblk[0:n, K % XB, :], ALU.max, ALU.add).then_inc(s_rd, 1)

                def add_x():
                    eng.wait_ge(s_rd, K + 1)
                    eng.wait_ge(s_x0[k % 2], 16 * (k // 2 + 1))
                    eng.tensor_tensor(tt, tt, x0b[0:n, k % 2, :], ALU.add).then_inc(s_ax, 1)

                def stats():
                    eng.wait_ge(s_ax, k + 1)
                    op(eng.bn_stats(bst[0:n, k % 2, :], tt))

                def aggr():
                    wait_own()
                    if k >= 2:
                        eng.wait_ge(s_sq, k - 1)
                    eng.bn_aggr(mv[0:n, k % 2, :], bst[0:n, k % 2, :]).then_inc(s_st, 1)

                def pause():
                    pass

                def recip():
                    eng.wait_ge(s_sq, k + 1)
                    if k >= 2:
                        eng.wait_ge(s_no, k - 1)
                    op(eng.reciprocal(rs[0:n, k % 2, :], sd[0:n, k % 2, :]))

                def shift():
                    wait_own()
                    eng.wait_ge(s_st, k + 1)
                    eng.scalar_tensor_tensor(nm[0:n, k % 2, :], mv[0:n, k % 2, 0:1], -1.0, rs[0:n, k % 2, :],
                                             ALU.mult, ALU.mult).then_inc(s_nm, 1)

                ops = [first, mean0, mean1, mean2, residual]
                return ops if l < L - 1 else ops + [add_x, stats, aggr, pause, recip, shift]

            def count_ops(k, i):
                v = inv[:, 3 * k:3 * k + 3]
                if i == 0:
                    eng.wait_ge(s_hc, acc_by(k))
                    if k == 0:
                        eng.tensor_copy(cnt[:, :], pH[:, 0:148]).then_inc(s_cd, 1)
                    elif acc_by(k) > acc_by(k - 1):
                        eng.wait_ge(s_cd, k)
                        eng.wait_ge(s_cm, k)
                        eng.tensor_tensor(cnt[:, 3 * k:148], cnt[:, 3 * k:148], pH[:, 3 * k:148],
                                          ALU.add).then_inc(s_cd, 1)
                    else:
                        eng.wait_ge(s_cd, k)
                        eng.tensor_copy(cnt[:, 3 * k:148], cnt[:, 3 * k:148]).then_inc(s_cd, 1)
                elif i == 1:
                    d = pA[starts[k] % 2]
                    eng.wait_ge(s_cm, k + 1)
                    eng.tensor_copy(cd[:, k % 2, :], d[:, 384:388]).then_inc(s_inv, 1)
                elif i == 2:
                    eng.wait_ge(s_inv, 4 * k + 1)
                    eng.tensor_tensor(v, cd[:, k % 2, 1:4], cd[:, k % 2, 0:3], ALU.subtract).then_inc(s_inv, 1)
                elif i == 3:
                    eng.wait_ge(s_inv, 4 * k + 2)
                    eng.tensor_scalar(v, v, 1.0, None, ALU.max).then_inc(s_inv, 1)
                else:
                    eng.wait_ge(s_inv, 4 * k + 3)
                    eng.reciprocal(v, v).then_inc(s_inv, 1)

            steps = [0] * TB
            bases = {}
            def fast():
                for l in range(L):
                    todo = {}
                    for q in range(-6, end):
                        Q = l * NP + q
                        if 0 <= q < NP and q % 4 == 0:
                            w = min(8, NT - 2 * q)
                            _, vals = nc.values_load_multi_w_load_instructions(
                                brow[32 * (2 * q // BR):32 * (2 * q // BR) + 1,
                                     2 * q % BR:2 * q % BR + w], engines=[DVE], min_val=0, max_val=R * (N - 1),
                                skip_runtime_bounds_check_because="three times a node's number")
                            bases.update({2 * q + i: v for i, v in enumerate(vals)})
                        if 0 <= q < NP:
                            for i in range(2):
                                n = 2 * Q + i
                                eng.wait_ge(s_g[n % XR], 16 * (n // XR + 1))
                            eng.wait_ge(s_e, Q + 1)
                            v = xg[:, (2 * Q) % XR:(2 * Q) % XR + 2, :]
                            eng.tensor_tensor(v, v, pE[Q % 2][:, :].rearrange("p (i d) -> p i d", i=2),
                                              ALU.mult).then_inc(s_m, 1)
                        if q == 2 and l:
                            eng.wait_ge(s_z, NB * l)
                        if 0 <= q - 2 < NP:
                            add_sums(l, q - 2, 0)
                        if 0 <= q < NP and q % 2 == 0:
                            selectors(l, q)
                        if l == 0 and (q + 6) // 2 < NG:
                            split((q + 6) // 2, q % 2)
                        for k in list(todo):
                            todo[k].pop(0)()
                            if not todo[k]:
                                del todo[k]
                        for k in starting(q, 2):
                            todo[k] = block_ops(l, k)
                        if l == 0:
                            for i, lag in ((0, -1), (1, 2), (3, 3)):
                                for k in starting(q, lag):
                                    count_ops(k, i)
                        if 0 <= q - 2 < NP:
                            add_sums(l, q - 2, 1)
                        if l == 0:
                            for i, lag in ((2, 2), (4, 3)):
                                for k in starting(q, lag):
                                    count_ops(k, i)
                assert not todo

            both(eng, "vector", fast)


_INS = ["x", "src", "dst", "edge_attr_32", "edge_type_3", "L0_gnn_weights", "L0_gnn_roots", "L0_gnn_biases",
        "L0_gnn_edge_w", "L0_gnn_edge_b"]


def kernel(**inputs):
    import numpy as _np
    import concourse.bacc as _bacc
    from concourse import mybir as _mybir
    from concourse.bass_utils import run_bass_kernel_spmd as _run

    nc = _bacc.Bacc("TRN2", target_bir_lowering=False, num_devices=1)
    arrays, args = {}, []
    for name in _INS:
        a = _np.ascontiguousarray(inputs[name])
        arrays[f"in_{name}_dram"] = a
        args.append(nc.dram_tensor(f"in_{name}_dram", a.shape, _mybir.dt.from_np(a.dtype), kind="ExternalInput").ap())
    due = block_limits()
    arrays["in_due_dram"] = due
    args.append(nc.dram_tensor("in_due_dram", due.shape, _mybir.dt.float32, kind="ExternalInput").ap())
    out = nc.dram_tensor("out_0_dram", (6250, 256), _mybir.dt.float32, kind="ExternalOutput").ap()
    gnn_program(nc, *args, out)
    r = _run(nc, [arrays], core_ids=[0])
    return r.results[0]["out_0_dram"]
```

```python
import concourse.bass as bass
from concourse import mybir
from contextlib import ExitStack


def plan():
    rest = [g for g in range(194) if not 13 <= g < 22]
    order = [rest[i // 2] if i % 2 == 0 else rest[-1 - i // 2] for i in range(len(rest))]
    order += list(range(13, 22)) + [194, 195]
    place = [4 * order.index(j // 4) + j % 4 for j in range(782)]

    def tile(node, way):
        u = min(1.0, max(0.0, node / 6250.0)) ** 0.5
        return min(782.0, max(0.0, 781.25 * u + way * 6 * (100000 * u * (1 - u)) ** 0.5 / 128))

    spans = [(int(tile(128 * k - 32, -1)) if k else 0, min(782, int(tile(128 * (k + 1), 1)) + 1)) for k in range(49)]
    ready = sorted((max(place[a:b]) // 2 + 3, k) for k, (a, b) in enumerate(spans))
    starts, last = [], -4
    for i, (q, k) in enumerate(ready):
        q = max(q, last + (6 if last < 380 else 4 if q < 390 else 2))
        q += q % 2 if q < 390 else 0
        starts.append(q)
        last = q
    first = []
    for g in range(196):
        near = [k for k in range(49) if tile(128 * (k + 1), 1) >= 4 * g]
        first.append(min(near[0] if near else 48, 45))
    return order, place, spans, [k for _, k in ready], starts, first


def block_limits():
    import numpy as np

    _, place, spans, blocks, starts, first = plan()
    limits = np.zeros((2, 7 * 128), np.float32)
    limits[1] = 1e9
    for j in range(782):
        limits[0, j] = 128 * first[j // 4]
        if first[j // 4] + 4 < 49:
            limits[1, j] = 128 * (first[j // 4] + 4) - 32
    for k, q in zip(blocks, starts):
        for j in range(782):
            if place[j] >= 2 * (q - 2):
                if j < spans[k][0]:
                    limits[1, j] = min(limits[1, j], 128 * k - 32)
                else:
                    limits[0, j] = max(limits[0, j], 128 * (k + 1))
    return np.ascontiguousarray(limits.reshape(2, 7, 128).transpose(2, 0, 1))


def gnn_program(nc, x_in, src, dst, edge_attr, edge_type, weights, roots, biases, edge_w, edge_b, due, out):
    F32, F32R, BF16, I32 = mybir.dt.float32, mybir.dt.float32r, mybir.dt.bfloat16, mybir.dt.int32
    ALU = mybir.AluOpType
    ACT = mybir.ActivationFunctionType
    AX = mybir.AxisListType
    DVE = mybir.EngineType.DVE

    N, E, D, R, L = 6250, 100000, 256, 3, 3
    NT = 782
    LAST = E - 128 * (NT - 1)
    NP = NT // 2
    CH = 7
    CL = NT - 128 * (CH - 1)
    WN = 32
    WK = WN * R
    ACC = N * R + WK
    NB = 49
    NLAST = N - 128 * (NB - 1)
    NG = NQ = 196
    XR, SR, TR, AR = 12, 8, 3, 6
    XB, XT, TB = 4, 2, 4
    PAD = 1000000
    BR = 448
    HW = 12
    HIGH = -4096

    x1 = nc.dram_tensor("x1", (N, D), F32).ap()
    x2 = nc.dram_tensor("x2", (N, D), F32).ap()
    attr_t = nc.dram_tensor("attr_t", (NG, 64, 512), F32).ap()
    HR = 128 * R * NB
    sums = nc.dram_tensor("sums", (HR + 128, D), F32).ap()
    xs = [x_in, x1, x2, out]

    order, _, _, blocks, starts, first = plan()

    def rows(k):
        return 128 if blocks[k] < NB - 1 else NLAST

    def tiles_of(g):
        return 4 if g < NG - 1 else NT - 4 * (NG - 1)

    def ring(l, i, depth, per):
        n = l * per + i
        return n % depth, n // depth + 1

    ctx = ExitStack()
    with ctx:
        def sb(name, shape, dt=F32):
            return ctx.enter_context(nc.sbuf_tensor(name, shape, dt))

        def sem(name):
            return ctx.enter_context(nc.semaphore(name))

        def sems(name, n):
            return [sem(f"{name}{i}") for i in range(n)]

        acc = sb("acc", [128, 2, ACC])
        accf = acc[:, :, :].rearrange("p h k -> p (h k)")
        idx = sb("idx", [128, NT], I32)
        kr = sb("kr", [128, NT], BF16)
        lo = sb("lo", [128, NT])
        hb = sb("hb", [128, NT], BF16)
        xg = sb("xg", [128, XR, D])
        S = sb("S", [128, SR, WK])
        at = sb("at", [128, TR, 512], F32R)
        hs = sb("hs", [128, 3, 4, 64])
        W = sb("W", [128, 8, D])
        bias = sb("bias", [128, D])
        wsb = sb("wsb", [128, 2, D], F32R)
        iota = sb("iota", [128, 148], BF16)
        ident = sb("ident", [128, 128])
        oh_a = sb("oh_a", [128, AR, 128], BF16)
        oh_b = sb("oh_b", [128, SR, HW], BF16)
        inv = sb("inv", [128, 147])
        cnt = sb("cnt", [128, 148])
        diff = sb("diff", [128, 128])
        brow = sb("brow", [33, BR], I32)
        base = sb("base", [128, CH])
        duet = sb("duet", [128, 2, CH])
        bad = sb("bad", [128, 2])
        flag = sb("flag", [1, 1], I32)
        mask = sb("mask", [128, 1], I32)
        zcol = sb("zcol", [128, 1])
        ones = sb("ones", [128, 1])
        eps = sb("eps", [128, 1])
        xblk = sb("xblk", [128, XB, D])
        xT = sb("xT", [128, XT, D])
        t = sb("t", [128, TB, D])
        x0b = lo[:, 0:2 * D].rearrange("p (i d) -> p i d", i=2)
        bst = sb("bst", [128, 2, 6])
        mv = sb("mv", [128, 2, 2])
        sd = sb("sd", [128, 2, 1])
        rs = sb("rs", [128, 2, 1])
        nm = duet[:, 0, 0:2].unsqueeze(2)

        P0 = 2 * ACC - 5 * 896 - D
        prep = [accf[:, P0 + 896 * i:P0 + 896 * (i + 1)] for i in range(5)]
        p_src = prep[0].bitcast(I32)
        p_f, p_rel, p_off, p_in = prep[1:5]
        Wf = W[:, :, :].rearrange("p m d -> p (m d)")
        p_dst, p_typ, p_hb = Wf[:, 0:896].bitcast(I32), Wf[:, 896:1792].bitcast(I32), Wf[:, 896:1792]
        p_lo = t[:, :, :].rearrange("p i d -> p (i d)")[:, 0:896]
        p_high = p_src[:, 0:D].bitcast(F32)
        Z = [0, 7200, 25200, 27700, 30300, P0, 2 * ACC]
        p_ew = accf[:, P0 + 5 * 896:P0 + 5 * 896 + D]

        def c3(p):
            return p.rearrange("q (c p) -> q c p", p=128)

        bank = [ctx.enter_context(nc.psum_tensor(f"bank{i}", [128, 512], F32)) for i in range(8)]
        pE = bank[0:2]
        pA = bank[2:4]
        pT = bank[4]
        pH = bank[5]
        pD = bank[6:8]

        s_pad, s_cst, s_id, s_zc, s_one, s_ez = (sem(n) for n in (
            "s_pad", "s_cst", "s_id", "s_zc", "s_one", "s_ez"))
        s_src, s_dst, s_typ, s_ew, s_due = (sem(n) for n in ("s_src", "s_dst", "s_typ", "s_eww", "s_due"))
        s_pf, s_pt, s_pc, s_idx, s_pca, s_wsb = (sem(n) for n in ("s_pf", "s_pt", "s_pc", "s_idx", "s_pca", "s_wsb"))
        s_ch = sem("s_ch")
        s_z0 = sem("s_z0")
        s_flag = sem("s_flag")
        s_g = sems("s_g", XR)
        s_e, s_m, s_r, s_S, s_sc, s_acc = (sem(n) for n in ("s_e", "s_m", "s_r", "s_S", "s_sc", "s_acc"))
        s_an = sems("s_an", 3)
        s_hi, s_lo, s_tr, s_atc = sem("s_hi"), sem("s_lo"), sem("s_tr"), sem("s_atc")
        s_ao = sems("s_ao", TR)
        s_at = sems("s_at", TR)
        s_oh, s_ob, s_cn, s_cm, s_inv, s_df = (sem(n) for n in (
            "s_oh", "s_ob", "s_cn", "s_cm", "s_inv", "s_df"))
        s_w = sem("s_w")
        s_xl = sems("s_xl", XB)
        s_x0 = sems("s_x0", 2)
        s_xt, s_xc, s_d0, s_d1, s_f0, s_f1, s_nm, s_z = (sem(n) for n in (
            "s_xt", "s_xc", "s_d0", "s_d1", "s_f0", "s_f1", "s_nm", "s_z"))
        s_rd, s_ax = sem("s_rd"), sem("s_ax")
        s_dc = sems("s_dc", TB)
        s_st, s_sq, s_no = sem("s_st"), sem("s_sq"), sem("s_no")
        s_xo = sems("s_xo", TB)

        producers = {"load": ("sync", 16), "swdge0": ("gpsimd", 16), "swdge1": ("gpsimd", 16),
                     "swdge2": ("gpsimd", 16), "pool": ("gpsimd", 1), "act": ("scalar", 1),
                     "pe": ("tensor", 1), "dve": ("vector", 1)}
        s_gen = {p: sem(f"s_gen_{p}") for p in producers}
        s_turn = {p: sem(f"s_turn_{p}") for p in ("sync", "gpsimd", "scalar", "tensor", "vector")}

        block = ctx.enter_context(nc.Block())

        def uses(l, i, depth, per):
            return len(range(i, l * per, depth))

        def tile(n):
            return 4 * order[n // 4] + n % 4

        def starting(q, lag):
            return [k for k in range(NB) if starts[k] + lag == q]

        def wide(l, k):
            return l == 0 and k < NB - 4 and starts[k + 1] - starts[k] >= 6

        def turn_step(k):
            return starts[k] - (2 if k < NB - 2 else 4)

        def mix_step(l, k, m):
            if k == NB - 2:
                return starts[k] + (-1, 0, 1, 1)[m]
            if m == 0 and k == NB - 1:
                return turn_step(k) + 2
            return starts[k] + (2 * m if wide(l, k) else 1 + m)

        def products(k, m):
            b = pD[m // 2] if k < NB - 1 else pE[m // 2]
            return b[0:rows(k), 256 * (m % 2):256 * (m % 2) + 256]

        def acc_by(k):
            return min(NT, 2 * (starts[k] - 2))

        def slot(l, j):
            return 4 * ((l * NQ + j // 4) % (SR // 4)) + j % 4

        end = starts[-1] + 16

        G_x, G_sum = xg[:, 0, :], xg[:, 3, :]
        G_w, G_at = xg[0:33, 1, :], xg[0:33, 2, 0:128]
        G_eq, G_eqb, G_tri = xg[:, 4, 0:128], xg[:, 4, 128:256], xg[:, 5, 0:128]
        G_h = xg[:, 6:9, :]
        G_key, G_lo, G_hb, G_bef, G_ok, G_row, G_dump = (xg[:, 9, c:c + 1] for c in range(7))
        G_inv = xg[:, 9, 8:11]
        G_src, G_dst, G_node, G_hi, G_typ = (xg[:, 9, c:c + 1].bitcast(I32) for c in range(12, 17))
        G_one = xg[:, 5, 128:256].bitcast(BF16)[:, 0:147]
        G_an = hs[:, 0, 0, 0:32]
        G_T = t[:, 0:4, :].rearrange("p a (b c) -> p (a b) c", c=128)
        G_t, G_x0, G_xb = xT[:, 0, :], xT[:, 1, :], xblk[:, 0, :]
        G_pk, G_pc = bank[0][:, 256:384], pH[:, 0:147]

        def start_steps():
            return [
                ("load", lambda e, i: e.dma_start(G_w[0:32, :], edge_w)),
                ("load", lambda e, i: e.dma_start(G_w[32:33, :], edge_b.rearrange("(a n) -> a n", a=1))),
                ("dve", lambda e, i: e.memset(G_at[32:33, :], 1.0)),
                ("dve", lambda e, i: e.memset(G_an, 0.0)),
                ("dve", lambda e, i: e.memset(inv[:, :], 0.0)),
                ("pool", lambda e, i: e.memset(G_tri, 1.0)),
                ("pool", lambda e, i: e.affine_select(out=G_tri, in_=G_tri, compare_op=ALU.is_gt, fill=0.0, base=0,
                                                      pattern=[[-1, 128]], channel_multiplier=1)),
                ("pool", lambda e, i: e.iota(G_dump, [[0, 1]], base=HR, channel_multiplier=1,
                                             allow_small_or_imprecise_dtypes=True)),
            ]

        def layer_steps(l):
            half = (HR + 128) // 2
            zero = [("load", lambda e, i, h=h: e.dma_start(
                sums[half * h:half * (h + 1), :].rearrange("(p r) d -> p (r d)", p=128),
                accf[:, 0:half * D // 128])) for h in range(2)]
            return zero + [("load", lambda e, i, r=r: e.dma_start(
                W[:, 2 * r:2 * r + 2, :],
                (weights[l, r] if r < R else roots[l]).rearrange("(h p) o -> p h o", p=128))) for r in range(R + 1)] + [
                ("load", lambda e, i: e.dma_start(bias[:, :], biases[l:l + 1, :].broadcast_to([128, D])))]

        def col(a, i):
            return a[:, i:i + 1] if isinstance(i, int) else a[:, bass.ds(i, 1)]

        def edge_steps(l, n):
            steps = [
                ("load", lambda e, i: e.dma_start(G_an[0:n, :], edge_attr[bass.ds(i * 128, n), :])),
                ("pe", lambda e, i: e.transpose(pT[0:32, 0:128], G_an, ident[:, :])),
                ("act", lambda e, i: e.activation(G_at[0:32, :], pT[0:32, 0:128], ACT.Copy)),
                ("pe", lambda e, i: e.matmul(pE[0][:, 0:256], G_at, G_w, start=True, stop=True)),
                ("dve", lambda e, i: e.tensor_copy(G_src, col(idx, i))),
                ("dve", lambda e, i: e.tensor_copy(G_lo, col(lo, i))),
                ("load", lambda e, i: e.dma_start(G_node[0:n, :], dst[bass.ds(i * 128, n)]
                                                  .rearrange("(p a) -> p a", a=1))),
                ("load", lambda e, i: e.dma_start(G_typ[0:n, :], edge_type[bass.ds(i * 128, n)]
                                                  .rearrange("(p a) -> p a", a=1))),
                ("dve", lambda e, i: e.tensor_scalar(G_hi, G_node, 7, None, ALU.logical_shift_right)),
                ("dve", lambda e, i: e.scalar_tensor_tensor(G_hb, G_hi, 3.0, G_typ, ALU.mult, ALU.add)),
                (f"swdge{l}", lambda e, i: e.indirect_dma_start(
                    out=G_x, out_offset=None, in_=xs[l],
                    in_offset=bass.IndirectOffsetOnAxis(ap=G_src, axis=0))),
                ("dve", lambda e, i: e.tensor_tensor(G_x, G_x, pE[0][:, 0:256], ALU.mult)),
                ("act", lambda e, i: e.activation(G_x, G_x, ACT.Relu)),
                ("dve", lambda e, i: e.scalar_tensor_tensor(G_key, G_hb, 128.0, G_lo, ALU.mult, ALU.subtract)),
                ("dve", lambda e, i: e.tensor_scalar(G_key, G_key, 0.5, None, ALU.add)),
                ("pe", lambda e, i: e.matmul(G_pk, G_key.to_broadcast([128, 128]), ident[:, :],
                                             start=True, stop=True)),
                ("dve", lambda e, i: e.tensor_scalar(G_eq, G_pk, G_key, None, ALU.is_equal)),
                ("dve", lambda e, i: e.tensor_tensor(G_eqb, G_eq, G_tri, ALU.mult)),
                ("dve", lambda e, i: e.tensor_reduce(G_bef, G_eqb, AX.X, ALU.add)),
                ("dve", lambda e, i: e.tensor_scalar(G_ok, G_key, float(HR), None, ALU.is_lt)),
                ("dve", lambda e, i: e.scalar_tensor_tensor(G_ok, G_bef, 0.5, G_ok, ALU.is_lt, ALU.mult)),
                ("dve", lambda e, i: e.tensor_tensor(G_row, G_key, G_dump, ALU.subtract)),
                ("dve", lambda e, i: e.tensor_tensor(G_row, G_row, G_ok, ALU.mult)),
                ("dve", lambda e, i: e.tensor_tensor(G_row, G_row, G_dump, ALU.add)),
                ("dve", lambda e, i: e.tensor_copy(G_dst, G_row)),
                ("pe", lambda e, i: e.matmul(pA[0][:, 0:256], G_eq, G_x, start=True, stop=True)),
                ("act", lambda e, i: e.activation(G_sum, pA[0][:, 0:256], ACT.Copy)),
                (f"swdge{l}", lambda e, i: e.indirect_dma_start(
                    out=sums, out_offset=bass.IndirectOffsetOnAxis(ap=G_dst, axis=0), in_=G_sum, in_offset=None,
                    compute_op=ALU.add, oob_is_err=True)),
            ]
            if l == 0:
                steps += [
                    ("dve", lambda e, i: e.tensor_scalar(oh_a[:, 0, :], iota[:, 1:129], G_lo, 0.5, ALU.add,
                                                         ALU.is_equal)),
                    ("dve", lambda e, i: e.tensor_scalar(G_one, iota[:, 1:148], G_hb, None, ALU.is_equal)),
                    ("pe", lambda e, i: e.matmul(G_pc, oh_a[:, 0, :], G_one, start=True, stop=True)),
                    ("dve", lambda e, i: e.tensor_tensor(inv[:, :], inv[:, :], G_pc, ALU.add)),
                ]
            return steps

        def count_steps():
            return [
                ("dve", lambda e, i: e.tensor_scalar(inv[:, :], inv[:, :], 1.0, None, ALU.max)),
                ("dve", lambda e, i: e.reciprocal(inv[:, :], inv[:, :])),
            ]

        def turn_all(e, n):
            for h in range(2):
                e.transpose(bank[0][:, 128 * h:128 * h + n], G_xb[0:n, 128 * h:128 * h + 128], ident[0:n, 0:n])
            for m in range(2, 8):
                ins = e.transpose(bank[m // 4][:, 128 * (m % 4):128 * (m % 4) + 128],
                                  G_h[:, m // 2 - 1, 128 * (m % 2):128 * (m % 2) + 128], ident[:, :])
            return ins

        def mix_all(e, n):
            for m in range(4):
                for h in range(2):
                    ins = e.matmul(pD[m // 2][0:n, 256 * (m % 2):256 * (m % 2) + 256], G_T[:, 2 * m + h, 0:n],
                                   W[:, 2 * ((m - 1) % 4) + h, :], start=(h == 0), stop=(h == 1))
            return ins

        def node_steps(l, n):
            tt = G_t[0:n, :]
            steps = [
                ("load", lambda e, i: e.dma_start(G_h, sums[bass.ds(i * (3 * 128), 3 * 128), :]
                                                  .rearrange("(r p) d -> p r d", p=128))),
                ("load", lambda e, i: e.dma_start(G_xb[0:n, :], xs[l][bass.ds(i * 128, n), :])),
                ("pe", lambda e, i: turn_all(e, n)),
                ("act", lambda e, i: e.activation(G_T[:, 0:2, 0:n], bank[0][:, 0:256]
                                                  .rearrange("p (a c) -> p a c", c=128)[:, :, 0:n], ACT.Copy)),
                ("act", lambda e, i: e.activation(G_T[:, 2:4, :], bank[0][:, 256:512]
                                                  .rearrange("p (a c) -> p a c", c=128), ACT.Copy)),
                ("act", lambda e, i: e.activation(G_T[:, 4:8, :], bank[1][:, :]
                                                  .rearrange("p (a c) -> p a c", c=128), ACT.Copy)),
                ("pe", lambda e, i: mix_all(e, n)),
                ("dve", lambda e, i: e.tensor_copy(G_inv, inv[:, bass.ds(i * 3, 3)])),
                ("dve", lambda e, i: e.tensor_tensor(tt, pD[0][0:n, 0:256], bias[0:n, :], ALU.add)),
            ] + [
                ("dve", lambda e, i, m=m: e.scalar_tensor_tensor(
                    tt, pD[m // 2][0:n, 256 * (m % 2):256 * (m % 2) + 256], G_inv[0:n, m - 1:m], tt,
                    ALU.mult, ALU.add)) for m in (1, 2, 3)
            ] + [
                ("dve", lambda e, i: e.scalar_tensor_tensor(tt, tt, 0.0, G_xb[0:n, :], ALU.max, ALU.add)),
            ]
            if l == L - 1:
                b, m, d, r = bst[0:n, 0, :], mv[0:n, 0, :], sd[0:n, 0, :], rs[0:n, 0, :]
                steps += [
                    ("load", lambda e, i: e.dma_start(G_x0[0:n, :], x_in[bass.ds(i * 128, n), :])),
                    ("dve", lambda e, i: e.tensor_tensor(tt, tt, G_x0[0:n, :], ALU.add)),
                    ("dve", lambda e, i: e.bn_stats(b, tt)),
                    ("dve", lambda e, i: e.bn_aggr(m, b)),
                    ("act", lambda e, i: e.activation(d, m[:, 1:2], ACT.Sqrt, bias=eps[0:n, :])),
                    ("dve", lambda e, i: e.reciprocal(r, d)),
                    ("dve", lambda e, i: e.tensor_scalar(tt, tt, m[:, 0:1], r, ALU.subtract, ALU.mult)),
                ]
            return steps + [("load", lambda e, i: e.dma_start(xs[l + 1][bass.ds(i * 128, n), :], tt))]

        def general(eng, name):
            done = dict.fromkeys(producers, 0)
            last = [None]

            def phase(steps, i0=0, times=1):
                per = {p: producers[p][1] * sum(s[0] == p for s in steps) for p in producers}

                def issue(i, turn):
                    now = dict(done)
                    prev = (steps[-1][0], now[steps[-1][0]] + turn * per[steps[-1][0]])
                    for p, step in steps:
                        now[p] += producers[p][1]
                        if producers[p][0] == name:
                            eng.wait_ge(s_gen[prev[0]], prev[1])
                            eng.sem_inc(s_turn[name], 1)
                            step(eng, i).then_inc(s_gen[p], producers[p][1])
                        prev = (p, now[p] + turn * per[p])

                mine = any(producers[p][0] == name for p, _ in steps)
                if producers[steps[0][0]][0] == name and last[0]:
                    eng.wait_ge(s_gen[last[0]], done[last[0]])
                if mine and times == 1:
                    issue(i0, 0)
                elif mine:
                    with eng.Fori(i0, i0 + times) as i:
                        issue(i, i - i0)
                for p in producers:
                    done[p] += times * per[p]
                last[0] = steps[-1][0]

            if name == "sync":
                eng.wait_ge(s_z0, 8)
                eng.wait_ge(s_pca, 4)
                eng.wait_ge(s_atc, 1)
                for i in range(XR):
                    eng.wait_ge(s_g[i], 16)
                for g in range(3):
                    eng.wait_ge(s_an[g], 16)
            phase(start_steps())
            for l in range(L):
                phase(layer_steps(l))
                phase(edge_steps(l, 128))
                phase(edge_steps(l, 128), 1, NT - 2)
                phase([("dve", lambda e, i: e.memset(G_node, PAD))])
                phase(edge_steps(l, LAST), NT - 1)
                if l == 0:
                    phase(count_steps())
                phase(node_steps(l, 128), 0, NB - 1)
                phase(node_steps(l, NLAST), NB - 1)
            if name == "sync":
                eng.wait_ge(s_gen["load"], done["load"])
                for l in range(L):
                    eng.wait_ge(s_gen[f"swdge{l}"], done[f"swdge{l}"])

        def both(eng, name, fast):
            eng.wait_ge(s_flag, 4)
            late = eng.value_load(flag[0:1, 0:1], min_val=0, max_val=128 * 128 * CH + 128 * CH)
            with eng.If(late == 0):
                fast()
            with eng.Else():
                general(eng, name)

        @block.sync
        def _(eng):
            eng.wait_ge(s_pad, 3)
            for p, a, s in ((p_src, src, s_src), (p_dst, dst, s_dst), (p_typ, edge_type, s_typ)):
                eng.dma_start(c3(p)[:, 0:CH - 1, :],
                              a[0:128 * 128 * (CH - 1)].rearrange("(c q p) -> q c p", q=128, p=128)).then_inc(s, 16)
                eng.dma_start(c3(p)[0:CL - 1, CH - 1, :],
                              a[128 * 128 * (CH - 1):128 * (NT - 1)].rearrange("(q p) -> q p", p=128)).then_inc(s, 16)
                eng.dma_start(c3(p)[CL - 1:CL, CH - 1, 0:LAST],
                              a[128 * (NT - 1):E].rearrange("(q p) -> q p", q=1)).then_inc(s, 16)
            eng.wait_ge(s_ez, 1)
            for i in range(2):
                eng.dma_start(p_ew[32 * i:32 * i + 32, :], edge_w).then_inc(s_ew, 16)
            eng.dma_start(p_ew[64:65, :], edge_b.rearrange("(a n) -> a n", a=1)).then_inc(s_ew, 16)
            eng.dma_start(duet[:, :, :], due).then_inc(s_due, 16)

            def load_weights(l):
                eng.wait_ge(s_pca, 4)
                if l:
                    eng.wait_ge(s_rd, NB * l)
                for i in range(R):
                    eng.dma_start(W[:, 2 * i:2 * i + 2, :],
                                  weights[l, i].rearrange("(h p) o -> p h o", p=128)).then_inc(s_w, 16)
                eng.dma_start(W[:, 6:8, :], roots[l].rearrange("(h p) o -> p h o", p=128)).then_inc(s_w, 16)
                eng.dma_start(bias[:, :], biases[l:l + 1, :].broadcast_to([128, D])).then_inc(s_w, 16)

            def load_attr(g):
                if g >= 3:
                    eng.wait_ge(s_tr, g - 2)
                if g < NG - 1:
                    eng.dma_start(hs[:, g % 3, :, 32:64], edge_attr[512 * order[g]:512 * (order[g] + 1), :]
                                  .rearrange("(j p) d -> p j d", p=128)).then_inc(s_an[g % 3], 16)
                else:
                    eng.dma_start(hs[:, g % 3, 0, 32:64], edge_attr[512 * g:512 * g + 128, :]).then_inc(s_an[g % 3], 16)
                    eng.dma_start(hs[0:LAST, g % 3, 1, 32:64], edge_attr[128 * (NT - 1):E, :]).then_inc(s_an[g % 3], 16)

            def keep_attr(g):
                w = 128 * tiles_of(g)
                eng.wait_ge(s_atc, g + 1)
                eng.dma_start(attr_t[g, :, 0:w], at[0:64, g % TR, 0:w].bitcast(F32)).then_inc(s_ao[g % TR], 16)

            def reload_attr(l, g):
                G = l * NG + g
                eng.wait_ge(s_e, l * NP + 2 * max(0, g - TR + 1))
                w = 128 * tiles_of(g)
                eng.dma_start(at[0:64, G % TR, 0:w].bitcast(F32), attr_t[g, :, 0:w]).then_inc(s_at[G % TR], 16)

            def load_x(l, k):
                K, n = NB * l + k, rows(k)
                if K >= XB:
                    eng.wait_ge(s_rd, K - XB + 1)
                eng.dma_start(xblk[0:n, K % XB, :], xs[l][128 * blocks[k]:128 * blocks[k] + n, :]).then_inc(s_xl[K % XB], 16)

            def load_x0(k):
                n = rows(k)
                if k >= 2:
                    eng.wait_ge(s_ax, k - 1)
                eng.dma_start(x0b[0:n, k % 2, :], x_in[128 * blocks[k]:128 * blocks[k] + n, :]).then_inc(s_x0[k % 2], 16)

            def store(l, k):
                K, n = NB * l + k, rows(k)
                if l < L - 1:
                    eng.wait_ge(s_rd, K + 1)
                else:
                    eng.wait_ge(s_no, k + 1)
                eng.dma_start(xs[l + 1][128 * blocks[k]:128 * blocks[k] + n, :], t[0:n, K % TB, :]).then_inc(s_xo[K % TB], 16)

            for g in range(3):
                load_attr(g)

            def fast():
                for l in range(L):
                    late = (13, 9, 15)[l]
                    for q in range(-4, end):
                        if l == 0 and q % 2 == 0:
                            if 3 <= q // 2 + 4 < NG:
                                load_attr(q // 2 + 4)
                            if 0 <= q // 2 < NG:
                                keep_attr(q // 2)
                        if l and q % 2 == 0 and q // 2 + 2 < NG:
                            reload_attr(l, q // 2 + 2)
                        if q == 0:
                            for i in range(TB if l else 0):
                                eng.wait_ge(s_xo[i], 16 * uses(l, i, TB, NB))
                            if l == 0:
                                load_weights(l)
                            for k in range(XB):
                                load_x(l, k)
                            if l == L - 1:
                                load_x0(0)
                                load_x0(1)
                        if q == 8 and l:
                            load_weights(l)
                        for k in starting(q, 8 if l else 12):
                            if k + XB < NB:
                                load_x(l, k + XB)
                        for k in starting(q, 9):
                            if l == L - 1 and k + 2 < NB:
                                load_x0(k + 2)
                        for k in starting(q, late):
                            store(l, k)
                    if l == 0:
                        for i in range(TR):
                            eng.wait_ge(s_ao[i], 16 * uses(1, i, TR, NG))
                for i in range(TB):
                    eng.wait_ge(s_xo[i], 16 * uses(L, i, TB, NB))

            both(eng, "sync", fast)

        @block.gpsimd
        def _(eng):
            eng.memset(c3(p_src)[:, CH - 1, :], 0).then_inc(s_pad, 1)
            eng.memset(c3(p_dst)[:, CH - 1, :], PAD).then_inc(s_pad, 1)
            eng.memset(c3(p_typ)[:, CH - 1, :], 0).then_inc(s_pad, 1)
            eng.memset(zcol[:, :], 0.0).then_inc(s_zc, 1)
            eng.memset(p_ew, 0.0).then_inc(s_ez, 1)
            eng.memset(ident[:, :], 0.0).then_inc(s_id, 1)
            eng.wait_ge(s_id, 1)
            eng.affine_select(out=ident[:, :], in_=ident[:, :], compare_op=ALU.not_equal, fill=1.0,
                              base=0, pattern=[[-1, 128]], channel_multiplier=1).then_inc(s_id, 1)
            eng.iota(iota[:, :], [[1, 148]], base=-1, channel_multiplier=0,
                     allow_small_or_imprecise_dtypes=True).then_inc(s_cst, 1)
            eng.memset(ones[:, :], 1.0).then_inc(s_cst, 1)
            eng.memset(mask[:, :], HIGH).then_inc(s_cst, 1)
            eng.memset(eps[:, :], 1e-5).then_inc(s_cst, 1)
            eng.memset(accf[:, Z[0]:Z[1]], 0.0).then_inc(s_z0, 1)

            def gather(l, j):
                n = l * NT + j
                if n >= XR:
                    eng.wait_ge(s_sc, 2 * ((n - XR) // 2 + 1))
                eng.indirect_dma_start(
                    out=xg[:, n % XR, :], out_offset=None, in_=xs[l],
                    in_offset=bass.IndirectOffsetOnAxis(ap=idx[:, tile(j):tile(j) + 1], axis=0)).then_inc(s_g[n % XR], 16)

            eng.wait_ge(s_idx, 2)
            for j in range(XR):
                gather(0, j)
            eng.memset(diff[:, :], 0.0).then_inc(s_df, 1)
            for i, (fill, b) in enumerate(((0.5, 0), (-0.5, 1), (0.5, -127))):
                eng.wait_ge(s_df, i + 1)
                eng.affine_select(out=diff[:, :], in_=diff[:, :], compare_op=ALU.not_equal, fill=fill,
                                  base=b, pattern=[[-1, 128]], channel_multiplier=1).then_inc(s_df, 1)
            eng.memset(accf[:, Z[4]:Z[5]], 0.0).then_inc(s_z0, 1)
            eng.wait_ge(s_pc, 3)
            eng.memset(accf[:, Z[5]:Z[6]], 0.0).then_inc(s_z0, 1)

            def fast():
                for l in range(L):
                    if l:
                        for i in range(TB):
                            eng.wait_ge(s_xo[i], 16 * uses(l, i, TB, NB))
                    for j in range(0 if l else XR, NT):
                        gather(l, j)

            both(eng, "gpsimd", fast)

        @block.scalar
        def _(eng):
            eng.wait_ge(s_zc, 1)
            for a in range(Z[1], Z[2], 6000):
                eng.activation(accf[:, a:a + 6000], zcol[:, 0:1].to_broadcast([128, 6000]), ACT.Copy).then_inc(s_z0, 1)

            def copies(dstn, b0, b1):
                eng.activation(dstn[:, 0:512], b0[:, 0:512], ACT.Copy).then_inc(s_pca, 1)
                eng.activation(dstn[:, 512:NT], b1[:, 0:NT - 512], ACT.Copy).then_inc(s_pca, 1)

            def high(g):
                eng.wait_ge(s_an[g % 3], 16 * (g // 3 + 1) + (16 if g == NG - 1 else 0))
                eng.activation(hs[:, g % 3, :, 0:32].bitcast(F32R), hs[:, g % 3, :, 32:64], ACT.Copy).then_inc(s_hi, 1)

            def attr_copy(g):
                w = 128 * tiles_of(g)
                eng.wait_ge(s_tr, g + 1)
                if g >= TR:
                    eng.wait_ge(s_e, 2 * (g - TR + 1))
                    eng.wait_ge(s_ao[g % TR], 16 * (g // TR))
                eng.activation(at[0:64, g % TR, 0:w], pT[0:64, 0:w], ACT.Copy).then_inc(s_atc, 1)

            eng.wait_ge(s_pt, 2)
            copies(lo, bank[4], bank[5])
            high(0)
            eng.activation(accf[:, Z[3]:Z[4]], zcol[:, 0:1].to_broadcast([128, Z[4] - Z[3]]),
                           ACT.Copy).then_inc(s_z0, 1)
            eng.wait_ge(s_pt, 5)
            copies(hb, bank[6], bank[7])
            attr_copy(0)

            def root(k):
                par, n = k % 2, rows(k)
                eng.wait_ge(s_st, k + 1)
                eng.activation(sd[0:n, par, :], mv[0:n, par, 1:2], ACT.Sqrt, bias=eps[0:n, :]).then_inc(s_sq, 1)

            def norm(k):
                K, par, n = NB * (L - 1) + k, k % 2, rows(k)
                eng.wait_ge(s_nm, k + 1)
                eng.activation(t[0:n, K % TB, :], t[0:n, K % TB, :], ACT.Identity, scale=rs[0:n, par, :],
                               bias=nm[0:n, par, :]).then_inc(s_no, 1)

            def fast():
                for l in range(L):
                    for q in range(-6, end):
                        Q = l * NP + q
                        if 0 <= q < NP:
                            eng.wait_ge(s_m, Q + 1)
                            v = xg[:, (2 * Q) % XR:(2 * Q) % XR + 2, :]
                            eng.activation(v, v, ACT.Relu).then_inc(s_r, 1)
                        if l == 0 and q % 2 == 0 and 1 <= (q + 2) // 2 < NG:
                            attr_copy((q + 2) // 2)
                        for k in [k for k in range(NB) if q == turn_step(k) + 1]:
                            K, n = NB * l + k, rows(k)
                            eng.wait_ge(s_xt, K + 1)
                            if K >= XT:
                                eng.wait_ge(s_d0, K - XT + 1)
                            eng.activation(xT[:, K % XT, :].rearrange("p (h n) -> p h n", h=2)[:, :, 0:n],
                                           pT[:, 0:256].rearrange("p (h n) -> p h n", h=2)[:, :, 0:n],
                                           ACT.Copy).then_inc(s_xc, 1)
                        if l == 0 and q % 2 == 0 and 1 <= (q + 6) // 2 < NG:
                            high((q + 6) // 2)
                        if l == 0 and 0 <= q + 1 < NP:
                            for j in (2 * q + 2, 2 * q + 3):
                                if j >= AR:
                                    eng.wait_ge(s_sc, j - AR + 1)
                                eng.activation(oh_a[:, j % AR, :], iota[:, 1:129], ACT.Sign,
                                               bias=lo[:, tile(j):tile(j) + 1]).then_inc(s_oh, 1)
                        if l < L - 1:
                            for k in starting(q, 5 if l else 7):
                                eng.wait_ge(s_d1, NB * l + k + 1)
                                a = 384 * blocks[k]
                                b = a + 384 if blocks[k] < NB - 1 else ACC
                                eng.activation(acc[:, :, a:b], zcol[:, 0:1].unsqueeze(2)
                                               .to_broadcast([128, 2, b - a]), ACT.Copy).then_inc(s_z, 1)
                        else:
                            for k in starting(q, 11):
                                root(k)
                            for k in starting(q, 14):
                                norm(k)

            both(eng, "scalar", fast)

        @block.tensor
        def _(eng):
            eng.wait_ge(s_id, 2)

            def turn(p, b0, b1):
                for c in range(CH):
                    q = 128 if c < CH - 1 else CL
                    b = b0 if c < 4 else b1
                    last = eng.transpose(b[:, 128 * (c % 4):128 * (c % 4) + q], c3(p)[0:q, c, :], ident[0:q, 0:q])
                last.then_inc(s_pt, 1)

            eng.wait_ge(s_pf, 1)
            turn(p_f, bank[0], bank[1])
            eng.wait_ge(s_pf, 2)
            turn(p_lo, bank[4], bank[5])
            eng.wait_ge(s_pf, 3)
            turn(p_rel, bank[2], bank[3])
            eng.wait_ge(s_idx, 2)
            eng.wait_ge(s_pf, 4)
            eng.wait_ge(s_cst, 2)
            for c in range(CH):
                eng.matmul(bank[c // 4][0:1, 128 * (c % 4):128 * (c % 4) + 128], base[:, c:c + 1], ident[:, :],
                           start=True, stop=True)
            eng.matmul(bank[1][0:1, 510:511], bad[:, 0:1], ones[:, :], start=True, stop=False)
            eng.matmul(bank[1][0:1, 510:511], bad[:, 1:2], ones[:, :], start=False, stop=True).then_inc(s_pt, 1)
            eng.wait_ge(s_pf, 5)
            turn(p_hb, bank[6], bank[7])
            turned = [0]

            def attr_turn(g):
                eng.wait_ge(s_lo, g + 1)
                eng.wait_ge(s_atc, g)
                eng.wait_ge(s_xc, turned[0])
                for i in range(tiles_of(g)):
                    last = eng.transpose(pT[0:64, 128 * i:128 * i + 128], hs[:, g % 3, i, :], ident[:, :])
                last.then_inc(s_tr, 1)

            eng.wait_ge(s_pca, 2)
            attr_turn(0)
            eng.wait_ge(s_pc, 2)
            eng.wait_ge(s_pca, 4)
            eng.wait_ge(s_wsb, 2)
            eng.wait_ge(s_one, 1)

            def edge_weights(l, q):
                Q = l * NP + q
                g = q // 2
                sl, times = ring(l, g, TR, NG)
                if q % 2 == 0:
                    if l == 0:
                        eng.wait_ge(s_atc, g + 1)
                    else:
                        eng.wait_ge(s_at[sl], 16 * (times - uses(1, sl, TR, NG)))
                if Q >= 2:
                    eng.wait_ge(s_m, Q - 1)
                if l and q == 0:
                    eng.wait_ge(s_f0, NB * l)
                    eng.wait_ge(s_f1, NB * l)
                for i in range(2):
                    c = 256 * (q % 2) + 128 * i
                    for p in range(2):
                        last = eng.matmul(pE[Q % 2][:, 256 * i:256 * i + 256], at[:, sl, c:c + 128],
                                          wsb[:, p, :], start=(p == 0), stop=(p == 1))
                last.then_inc(s_e, 1)

            def collect(l, q):
                V = l * NP + q
                eng.wait_ge(s_r, V + 1)
                if V >= 2:
                    eng.wait_ge(s_acc, 2 * (V - 1))
                eng.wait_ge(s_S, q // 2 + 1 + l * NQ)
                if l == 0:
                    eng.wait_ge(s_ob, q // 2 + 1)
                    eng.wait_ge(s_oh, 2 * V + 2)
                    for i in range(2):
                        eng.matmul(pA[V % 2][:, 384:384 + HW], oh_a[:, (2 * V + i) % AR, :],
                                   oh_b[:, slot(l, 2 * q + i), :], start=(i == 0), stop=(i == 1))
                for i in range(2):
                    n = 2 * V + i
                    for h in range(2):
                        last = eng.matmul(pA[V % 2][:, 192 * i + 96 * h:192 * i + 96 * h + 96],
                                          xg[:, n % XR, 128 * h:128 * h + 128], S[:, slot(l, 2 * q + i), :],
                                          start=True, stop=True)
                    last.then_inc(s_sc, 1)

            def count(k):
                if k == 0:
                    eng.wait_ge(s_df, 4)
                else:
                    eng.wait_ge(s_inv, 2 * k - 1)
                eng.wait_ge(s_cn, min(NP, starts[k] - 1))
                eng.matmul(pH[:, 4 * (k % 2):4 * (k % 2) + 3], diff[:, :], cnt[:, 3 * blocks[k]:3 * blocks[k] + 3],
                           start=True, stop=True).then_inc(s_cm, 1)

            def turn_x(l, k):
                K, n = NB * l + k, rows(k)
                eng.wait_ge(s_xl[K % XB], 16 * (K // XB + 1))
                if K:
                    eng.wait_ge(s_xc, K)
                if l == 0:
                    eng.wait_ge(s_atc, min(NG, turn_step(k) // 2 + 2))
                    turned[0] += 1
                for h in range(2):
                    last = eng.transpose(pT[:, 128 * h:128 * h + n], xblk[0:n, K % XB, 128 * h:128 * h + 128],
                                         ident[0:n, 0:n])
                last.then_inc(s_xt, 1)

            def mix(l, k, m):
                K, n = NB * l + k, rows(k)
                o = products(k, m)
                if k == NB - 1 and m == 0:
                    eng.wait_ge(s_m, (l + 1) * NP)
                if m == 0:
                    eng.wait_ge(s_xc, K + 1)
                if m == 0 and 0 < k < NB - 1:
                    eng.wait_ge(s_f0, K)
                if m == 0:
                    if k == 0:
                        eng.wait_ge(s_w, 80 * (l + 1))
                if m == 1:
                    eng.wait_ge(s_acc, l * NT + acc_by(k))
                if m == 2 and 0 < k < NB - 1:
                    eng.wait_ge(s_f1, K)
                for h in range(2):
                    r = m - 1
                    a = (acc[:, h, 384 * blocks[k] + r:384 * blocks[k] + r + 3 * (n - 1) + 1:3] if m
                         else xT[:, K % XT, 128 * h:128 * h + n])
                    last = eng.matmul(o, a, W[:, 2 * (r % 4) + h, :], start=(h == 0), stop=(h == 1))
                if m % 2:
                    last.then_inc(pair_done[m // 2], 1)

            pair_done = [s_d0, s_d1]
            def fast():
                for l in range(L):
                    for q in range(-3, end):
                        if 0 <= q + 1 < NP:
                            edge_weights(l, q + 1)
                        if l == 0:
                            for k in starting(q, 1):
                                count(k)
                        if 0 <= q - 1 < NP:
                            collect(l, q - 1)
                        for k in range(NB):
                            for m in range(R + 1):
                                if q == mix_step(l, k, m):
                                    mix(l, k, m)
                        if l == 0 and q % 2 and 1 <= (q + 3) // 2 < NG:
                            attr_turn((q + 3) // 2)
                        for k in range(NB):
                            if q == turn_step(k):
                                turn_x(l, k)

            both(eng, "tensor", fast)

        @block.vector
        def _(eng):
            chain = [0]

            def link(ins):
                chain[0] += 1
                ins.then_inc(s_ch, 1)
                eng.wait_ge(s_ch, chain[0])

            def split(g):
                raw, high = hs[:, g % 3, :, 32:64], hs[:, g % 3, :, 0:32]
                eng.wait_ge(s_hi, g + 1)
                eng.tensor_tensor(raw, raw, high, ALU.subtract).then_inc(s_lo, 1)

            eng.memset(at[64:128, :, :].bitcast(F32), 1.0).then_inc(s_one, 1)
            eng.memset(accf[:, Z[2]:Z[3]], 0.0).then_inc(s_z0, 1)
            link(eng.memset(cnt[:, :], 0.0))
            eng.wait_ge(s_src, 48)
            eng.tensor_copy(p_f, p_src).then_inc(s_pf, 1)
            eng.wait_ge(s_dst, 48)
            link(eng.tensor_scalar(p_lo.bitcast(I32), p_dst, 127, None, ALU.bitwise_and))
            link(eng.tensor_scalar(p_lo, p_lo.bitcast(I32), -1.0, 0.5, ALU.mult, ALU.add))
            eng.sem_inc(s_pf, 1)
            eng.wait_ge(s_pt, 1)
            eng.tensor_copy(idx[:, 0:512], bank[0][:, 0:512]).then_inc(s_idx, 1)
            eng.tensor_copy(idx[:, 512:NT], bank[1][:, 0:NT - 512]).then_inc(s_idx, 1)
            eng.wait_ge(s_typ, 48)
            link(eng.tensor_copy(p_f, p_dst))
            link(eng.tensor_reduce(base[:, :], c3(p_f), AX.X, ALU.min))
            link(eng.tensor_tensor(c3(p_off), c3(p_f), base[:, :].unsqueeze(2).to_broadcast([128, CH, 128]),
                                   ALU.subtract))
            link(eng.scalar_tensor_tensor(p_rel, p_off, 3.0, p_typ, ALU.mult, ALU.add))
            eng.sem_inc(s_pf, 1)
            link(eng.scalar_tensor_tensor(p_in, p_off, float(PAD) / 2, p_off, ALU.is_lt, ALU.mult))
            link(eng.tensor_reduce(bad[:, 0:1], p_in, AX.X, ALU.max))
            link(eng.tensor_scalar(bad[:, 0:1], bad[:, 0:1], float(WN), None, ALU.is_ge))
            eng.wait_ge(s_due, 16)
            link(eng.tensor_tensor(duet[:, 0, :], base[:, :], duet[:, 0, :], ALU.is_lt))
            link(eng.tensor_tensor(duet[:, 1, :], base[:, :], duet[:, 1, :], ALU.is_gt))
            link(eng.tensor_reduce(bad[:, 1:2], duet[:, :, :].rearrange("p a c -> p (a c)"), AX.X, ALU.add))
            eng.sem_inc(s_pf, 1)
            eng.wait_ge(s_ew, 48)
            eng.wait_ge(s_cst, 3)
            link(eng.tensor_tensor(p_high.bitcast(I32), p_ew.bitcast(I32), mask[:, :].to_broadcast([128, D]),
                                   ALU.bitwise_and))
            eng.tensor_copy(wsb[:, 0, :], p_high).then_inc(s_wsb, 1)
            eng.tensor_tensor(wsb[:, 1, :], p_ew, p_high, ALU.subtract).then_inc(s_wsb, 1)
            eng.wait_ge(s_wsb, 2)
            eng.wait_ge(s_pt, 3)
            eng.tensor_copy(kr[:, 0:512], bank[2][:, 0:512]).then_inc(s_pc, 1)
            eng.tensor_copy(kr[:, 512:NT], bank[3][:, 0:NT - 512]).then_inc(s_pc, 1)
            link(eng.tensor_scalar(p_dst, p_dst, 7, None, ALU.logical_shift_right))
            link(eng.scalar_tensor_tensor(p_hb, p_dst, 3.0, p_typ, ALU.mult, ALU.add))
            eng.sem_inc(s_pf, 1)
            split(0)
            eng.wait_ge(s_pt, 4)
            for a, b in ((brow[0:1, 0:BR], bank[0][0:1, 0:BR]),
                         (brow[32:33, 0:512 - BR], bank[0][0:1, BR:512]),
                         (brow[32:33, 512 - BR:BR], bank[1][0:1, 0:384])):
                eng.tensor_scalar(a, b, 3.0, None, ALU.mult).then_inc(s_flag, 1)
            eng.tensor_copy(flag[:, :], bank[1][0:1, 510:511]).then_inc(s_flag, 1)
            eng.wait_ge(s_pc, 2)
            eng.sem_inc(s_pc, 1)
            eng.wait_ge(s_cst, 4)
            eng.wait_ge(s_pca, 4)
            eng.wait_ge(s_flag, 4)

            def selectors(l, q):
                j, w = 2 * q, min(4, NT - 2 * q)
                c = tile(j)
                at4 = slot(l, j)
                if l or j >= SR:
                    eng.wait_ge(s_sc, l * NT + (j - 4 if j >= SR else 0 if j else -2))
                eng.tensor_tensor(S[:, at4:at4 + w, :], iota[:, 1:WK + 1].unsqueeze(1).to_broadcast([128, w, WK]),
                                  kr[:, c:c + w].unsqueeze(2).to_broadcast([128, w, WK]),
                                  ALU.is_equal).then_inc(s_S, 1)
                if l == 0:
                    f = 3 * first[c // 4]
                    eng.tensor_tensor(oh_b[:, at4:at4 + w, :],
                                      iota[:, 1 + f:1 + f + HW].unsqueeze(1).to_broadcast([128, w, HW]),
                                      hb[:, c:c + w].unsqueeze(2).to_broadcast([128, w, HW]),
                                      ALU.is_equal).then_inc(s_ob, 1)

            def add_sums(l, q, i):
                V = l * NP + q
                n = 2 * V + i
                if n == 0:
                    eng.wait_ge(s_z0, 8)
                eng.wait_ge(s_sc, 2 * V + 2)
                if n:
                    eng.wait_ge(s_acc, n)
                a = acc[:, :, bass.ds(bases.pop(2 * q + i), WK)]
                eng.tensor_tensor(a, a, pA[V % 2][:, 192 * i:192 * i + 192]
                                  .rearrange("p (h w) -> p h w", h=2), ALU.add).then_inc(s_acc, 1)

            def block_ops(l, k):
                K, n = NB * l + k, rows(k)
                i = K % TB
                tt = t[0:n, i, :]

                def wait_own():
                    eng.wait_ge(s_dc[i], steps[i])

                def op(ins):
                    steps[i] += 1
                    ins.then_inc(s_dc[i], 1)

                def mean(r):
                    m = r + 1
                    return eng.scalar_tensor_tensor(tt, products(k, m),
                                                    inv[0:n, 3 * blocks[k] + r:3 * blocks[k] + r + 1],
                                                    tt, ALU.mult, ALU.add)

                def first():
                    eng.wait_ge(s_d0, K + 1)
                    eng.wait_ge(s_xo[i], 16 * (K // TB))
                    op(eng.tensor_tensor(tt, products(k, 0), bias[0:n, :], ALU.add))

                def mean0():
                    wait_own()
                    eng.wait_ge(s_inv, 2 * min(K + 1, NB))
                    mean(0).then_inc(s_f0, 1)

                def mean1():
                    eng.wait_ge(s_f0, K + 1)
                    eng.wait_ge(s_d1, K + 1)
                    op(mean(1))

                def mean2():
                    wait_own()
                    mean(2).then_inc(s_f1, 1)

                def residual():
                    eng.wait_ge(s_f1, K + 1)
                    eng.scalar_tensor_tensor(tt, tt, 0.0, xblk[0:n, K % XB, :], ALU.max, ALU.add).then_inc(s_rd, 1)

                def add_x():
                    eng.wait_ge(s_rd, K + 1)
                    eng.wait_ge(s_x0[k % 2], 16 * (k // 2 + 1))
                    eng.tensor_tensor(tt, tt, x0b[0:n, k % 2, :], ALU.add).then_inc(s_ax, 1)

                def stats():
                    eng.wait_ge(s_ax, k + 1)
                    op(eng.bn_stats(bst[0:n, k % 2, :], tt))

                def aggr():
                    wait_own()
                    if k >= 2:
                        eng.wait_ge(s_sq, k - 1)
                    eng.bn_aggr(mv[0:n, k % 2, :], bst[0:n, k % 2, :]).then_inc(s_st, 1)

                def pause():
                    pass

                def recip():
                    eng.wait_ge(s_sq, k + 1)
                    if k >= 2:
                        eng.wait_ge(s_no, k - 1)
                    op(eng.reciprocal(rs[0:n, k % 2, :], sd[0:n, k % 2, :]))

                def shift():
                    wait_own()
                    eng.wait_ge(s_st, k + 1)
                    eng.scalar_tensor_tensor(nm[0:n, k % 2, :], mv[0:n, k % 2, 0:1], -1.0, rs[0:n, k % 2, :],
                                             ALU.mult, ALU.mult).then_inc(s_nm, 1)

                ops = [first, mean0, mean1, mean2, residual]
                if wide(l, k):
                    return [o for f in ops for o in (f, pause)]
                return ops if l < L - 1 else ops + [add_x, stats, aggr, pause, recip, shift]

            def add_counts(q):
                f = 3 * first[tile(2 * q) // 4]
                eng.wait_ge(s_cn, q)
                eng.wait_ge(s_cm, sum(p - 1 <= q for p in starts))
                eng.tensor_tensor(cnt[:, f:f + HW], cnt[:, f:f + HW], pA[q % 2][:, 384:384 + HW],
                                  ALU.add).then_inc(s_cn, 1)

            def count_ops(k, i):
                v = inv[:, 3 * blocks[k]:3 * blocks[k] + 3]
                if i == 0:
                    eng.wait_ge(s_cm, k + 1)
                    eng.tensor_scalar(v, pH[:, 4 * (k % 2):4 * (k % 2) + 3], 1.0, None, ALU.max).then_inc(s_inv, 1)
                else:
                    eng.wait_ge(s_inv, 2 * k + 1)
                    eng.reciprocal(v, v).then_inc(s_inv, 1)

            steps = [0] * TB
            bases = {}
            def fast():
                for l in range(L):
                    todo = {}
                    for q in range(-6, end):
                        Q = l * NP + q
                        if 0 <= q < NP and q % 2 == 0:
                            w, c = min(4, NT - 2 * q), tile(2 * q)
                            row, c = 32 * (c // BR), c % BR
                            _, vals = nc.values_load_multi_w_load_instructions(
                                brow[row:row + 1, c:c + w], engines=[DVE], min_val=0, max_val=R * (N - 1),
                                skip_runtime_bounds_check_because="three times a node's number")
                            bases.update({2 * q + i: v for i, v in enumerate(vals)})
                        if 0 <= q < NP:
                            for i in range(2):
                                n = 2 * Q + i
                                eng.wait_ge(s_g[n % XR], 16 * (n // XR + 1))
                            eng.wait_ge(s_e, Q + 1)
                            v = xg[:, (2 * Q) % XR:(2 * Q) % XR + 2, :]
                            eng.tensor_tensor(v, v, pE[Q % 2][:, :].rearrange("p (i d) -> p i d", i=2),
                                              ALU.mult).then_inc(s_m, 1)
                        if q == 2 and l:
                            eng.wait_ge(s_z, NB * l)
                        if 0 <= q - 2 < NP:
                            add_sums(l, q - 2, 0)
                        if 0 <= q < NP and q % 2 == 0:
                            selectors(l, q)
                        if l == 0 and q % 2 and 1 <= (q + 6) // 2 < NG:
                            split((q + 6) // 2)
                        for k in list(todo):
                            todo[k].pop(0)()
                            if not todo[k]:
                                del todo[k]
                        for k in range(NB):
                            if q == starts[k] + (2 if l == 0 or k != NB - 2 else 0):
                                todo[k] = block_ops(l, k)
                        if l == 0:
                            for i, lag in ((0, 2), (1, 3)):
                                for k in starting(q, lag):
                                    count_ops(k, i)
                            if 0 <= q - 2 < NP:
                                add_counts(q - 2)
                        if 0 <= q - 2 < NP:
                            add_sums(l, q - 2, 1)
                assert not todo

            both(eng, "vector", fast)


_INS = ["x", "src", "dst", "edge_attr_32", "edge_type_3", "L0_gnn_weights", "L0_gnn_roots", "L0_gnn_biases",
        "L0_gnn_edge_w", "L0_gnn_edge_b"]


def kernel(**inputs):
    import numpy as _np
    import concourse.bacc as _bacc
    from concourse import mybir as _mybir
    from concourse.bass_utils import run_bass_kernel_spmd as _run

    nc = _bacc.Bacc("TRN2", target_bir_lowering=False, num_devices=1)
    arrays, args = {}, []
    for name in _INS:
        a = _np.ascontiguousarray(inputs[name])
        arrays[f"in_{name}_dram"] = a
        args.append(nc.dram_tensor(f"in_{name}_dram", a.shape, _mybir.dt.from_np(a.dtype), kind="ExternalInput").ap())
    due = block_limits()
    arrays["in_due_dram"] = due
    args.append(nc.dram_tensor("in_due_dram", due.shape, _mybir.dt.float32, kind="ExternalInput").ap())
    out = nc.dram_tensor("out_0_dram", (6250, 256), _mybir.dt.float32, kind="ExternalOutput").ap()
    gnn_program(nc, *args, out)
    r = _run(nc, [arrays], core_ids=[0])
    return r.results[0]["out_0_dram"]
```
